# Optimizing a Trainium2 kernel written in Bass

```python
import numpy as np
import jax
import jax.numpy as jnp

def _softmax(x, axis=-1):
    return jax.nn.softmax(x, axis=axis)

def _gelu(x):
    return jax.nn.gelu(x, approximate=True)

def _silu(x):
    return jax.nn.silu(x)

def _sigmoid(x):
    return jax.nn.sigmoid(x)

def _layernorm(x, axis=-1, eps=1e-05):
    m = jnp.mean(x, axis=axis, keepdims=True)
    v = jnp.var(x, axis=axis, keepdims=True)
    return (x - m) / jnp.sqrt(v + eps)

def _scatter_add(tgt, idx, src, axis=0):
    return tgt.at[idx].add(src)

def _segment_sum(src, seg, n):
    return jax.ops.segment_sum(src, seg, n)
kernel_name = 'mk_adaln_d1_jaxref_r4_e5c3cb'

def setup_inputs(seed: int=0):
    np.random.seed(seed)
    _w = jnp.asarray

    def _L0_attn_setup():
        import jax, jax.numpy as jnp
        import numpy as np
        HEADS = 16
        DIM_HEAD = 64
        T_MAX = DIM_HEAD

        def _cope(q, sim, pos_emb):
            G = jax.nn.sigmoid(sim)
            P = jnp.flip(jnp.cumsum(jnp.flip(G, axis=-1), axis=-1), axis=-1)
            P = jnp.minimum(P, T_MAX - 1)
            P_floor = jnp.floor(P)
            P_ceil_i = jnp.ceil(P).astype(jnp.int32)
            P_floor_i = P_floor.astype(jnp.int32)
            E = jnp.einsum('bnc,ct->bnt', q, pos_emb)
            E_ceil = jnp.take_along_axis(E, P_ceil_i, axis=-1)
            E_floor = jnp.take_along_axis(E, P_floor_i, axis=-1)
            w = P - P_floor
            return w * E_ceil + (1.0 - w) * E_floor
        key = jax.random.key(seed)
        ks = jax.random.split(key, 6)
        B, N, D = (1, 512, 256)
        inner = HEADS * DIM_HEAD
        return {'x': jax.random.normal(ks[0], (B, N, D), dtype=jnp.float32), 'Wq': jax.random.normal(ks[1], (D, inner), dtype=jnp.float32) * 0.02, 'Wkv': jax.random.normal(ks[2], (D, 2 * inner), dtype=jnp.float32) * 0.02, 'Wout': jax.random.normal(ks[3], (inner, D), dtype=jnp.float32) * 0.02, 'b_out': jnp.zeros((D,), dtype=jnp.float32), 'pos_emb': jax.random.normal(ks[4], (DIM_HEAD, T_MAX), dtype=jnp.float32) * 0.02}
    _L0_attn_in = _L0_attn_setup()

    def _L0_ffn_setup():
        import jax, jax.numpy as jnp
        import numpy as np
        THRESHOLD = 0.1
        key = jax.random.key(seed)
        k1, k2, k3 = jax.random.split(key, 3)
        B, S, D, E = (4, 1024, 256, 8)
        inputs = jax.random.normal(k1, (B, S, D), dtype=jnp.float32)
        gate_w = jax.random.normal(k2, (D, E), dtype=jnp.float32) * 0.02
        gate_b = jnp.zeros((E,), dtype=jnp.float32)
        expert_w = jax.random.normal(k3, (E, D, D), dtype=jnp.float32) * 0.02
        expert_b = jnp.zeros((E, D), dtype=jnp.float32)
        return {'inputs': inputs, 'gate_w': gate_w, 'gate_b': gate_b, 'expert_w': expert_w, 'expert_b': expert_b}
    _L0_ffn_in = _L0_ffn_setup()
    _L0_c = _w((lambda *s: np.random.randn(*s).astype(np.float32) * 0.05)(4, 256))
    _L0_wmod = _w((lambda *s: np.random.randn(*s).astype(np.float32) * 0.05)(256, 6 * 256) * 256 ** (-0.5))
    _d = {'L0_attn_x': _L0_attn_in['x'], 'L0_attn_Wq': _L0_attn_in['Wq'], 'L0_attn_Wkv': _L0_attn_in['Wkv'], 'L0_attn_Wout': _L0_attn_in['Wout'], 'L0_attn_b_out': _L0_attn_in['b_out'], 'L0_attn_pos_emb': _L0_attn_in['pos_emb'], 'L0_ffn_gate_w': _L0_ffn_in['gate_w'], 'L0_ffn_gate_b': _L0_ffn_in['gate_b'], 'L0_ffn_expert_w': _L0_ffn_in['expert_w'], 'L0_ffn_expert_b': _L0_ffn_in['expert_b'], 'L0_c': _L0_c, 'L0_wmod': _L0_wmod}
    _x0 = _d['L0_attn_x']
    _d['L0_attn_x'] = jax.random.normal(jax.random.fold_in(jax.random.key(seed), 1), (4, 1024, 256), dtype=_x0.dtype)
    del _x0
    return _d

def reference(L0_attn_x, L0_attn_Wq, L0_attn_Wkv, L0_attn_Wout, L0_attn_b_out, L0_attn_pos_emb, L0_ffn_gate_w, L0_ffn_gate_b, L0_ffn_expert_w, L0_ffn_expert_b, L0_c, L0_wmod):

    def _L0_attn_ref(x, Wq, Wkv, Wout, b_out, pos_emb):
        import jax, jax.numpy as jnp
        import numpy as np
        HEADS = 16
        DIM_HEAD = 64
        T_MAX = DIM_HEAD

        def _cope(q, sim, pos_emb):
            G = jax.nn.sigmoid(sim)
            P = jnp.flip(jnp.cumsum(jnp.flip(G, axis=-1), axis=-1), axis=-1)
            P = jnp.minimum(P, T_MAX - 1)
            P_floor = jnp.floor(P)
            P_ceil_i = jnp.ceil(P).astype(jnp.int32)
            P_floor_i = P_floor.astype(jnp.int32)
            E = jnp.einsum('bnc,ct->bnt', q, pos_emb)
            E_ceil = jnp.take_along_axis(E, P_ceil_i, axis=-1)
            E_floor = jnp.take_along_axis(E, P_floor_i, axis=-1)
            w = P - P_floor
            return w * E_ceil + (1.0 - w) * E_floor
        B, N, D = x.shape
        h, d = (HEADS, DIM_HEAD)
        scale = d ** (-0.5)
        q = x @ Wq
        kv = x @ Wkv
        k, v = jnp.split(kv, 2, axis=-1)

        def to_heads(t):
            return t.reshape(B, N, h, d).transpose(0, 2, 1, 3).reshape(B * h, N, d)
        q, k, v = (to_heads(q), to_heads(k), to_heads(v))
        sim = jnp.einsum('bid,bjd->bij', q, k) * scale
        sim = sim + _cope(q, sim, pos_emb)
        attn = jax.nn.softmax(sim, axis=-1)
        out = jnp.einsum('bij,bjd->bid', attn, v)
        out = out.reshape(B, h, N, d).transpose(0, 2, 1, 3).reshape(B, N, h * d)
        return out @ Wout + b_out

    def _L0_ffn_ref(inputs, gate_w, gate_b, expert_w, expert_b):
        import jax, jax.numpy as jnp
        import numpy as np
        THRESHOLD = 0.1
        d = inputs.shape[-1]
        x = inputs.reshape(-1, d)
        gate_logits = jax.nn.softmax(x @ gate_w + gate_b, axis=-1)
        selected = (gate_logits >= THRESHOLD).astype(x.dtype)
        weights = gate_logits * selected
        wsum = jnp.sum(weights, axis=-1, keepdims=True)
        weights = weights / jnp.where(wsum == 0, jnp.ones_like(wsum), wsum)
        E = expert_w.shape[0]
        out = jnp.zeros((x.shape[0], expert_w.shape[-1]), dtype=x.dtype)
        for e in range(E):
            out = out + weights[:, e:e + 1] * (x @ expert_w[e] + expert_b[e])
        return out.reshape(*inputs.shape[:-1], out.shape[-1])
    x = L0_attn_x
    mod = (_silu(L0_c) @ L0_wmod).reshape(L0_c.shape[0], 6, 1, -1)
    sa, ca, ga, sb, cb, gb = (mod[:, 0], mod[:, 1], mod[:, 2], mod[:, 3], mod[:, 4], mod[:, 5])
    ga = (2 * (ga >= 0) - 1) * jnp.maximum(jnp.abs(ga), 0.25)
    gb = (2 * (gb >= 0) - 1) * jnp.maximum(jnp.abs(gb), 0.25)
    h = _layernorm(x, axis=-1) * (1 + ca) + sa
    x = x + ga * _L0_attn_ref(h, L0_attn_Wq, L0_attn_Wkv, L0_attn_Wout, L0_attn_b_out, L0_attn_pos_emb)
    h = _layernorm(x, axis=-1) * (1 + cb) + sb
    x = x + gb * _L0_ffn_ref(h, L0_ffn_gate_w, L0_ffn_gate_b, L0_ffn_expert_w, L0_ffn_expert_b)
    return x

_drawn_inputs = setup_inputs


def setup_inputs(seed=0):
    import zlib

    import numpy as np

    out = dict(_drawn_inputs(seed))
    spreads = {'L0_attn_b_out': (0.0, 0.337),
     'L0_ffn_gate_b': (0.0, 0.729),
     'L0_ffn_expert_b': (0.0, 0.711)}
    factors = {'L0_attn_Wq': 8.0,
     'L0_attn_Wkv': 8.0,
     'L0_attn_Wout': 8.0,
     'L0_attn_pos_emb': 8.0,
     'L0_ffn_gate_w': 2.692,
     'L0_ffn_expert_w': 2.769}
    for name, (base, spread) in spreads.items():
        noise = np.random.default_rng([zlib.crc32(name.encode()), seed]).standard_normal(out[name].shape)
        drawn = base * np.exp(spread * noise) if base else spread * noise
        out[name] = jnp.asarray(drawn.astype(out[name].dtype))
    for name, factor in factors.items():
        out[name] = (out[name] * factor).astype(out[name].dtype)
    return out
```

```python
import concourse.bass as bass
from concourse import mybir
from contextlib import ExitStack

FP32 = mybir.dt.float32
I16 = mybir.dt.int16
I32 = mybir.dt.int32
ALU = mybir.AluOpType
ACT = mybir.ActivationFunctionType
AX = mybir.AxisListType.X

B, N, D = 4, 1024, 256
H, DH = 16, 64
PTS = 64
CAP = float(PTS - 1)
KC = D // 128
TOK = B * N
PAIRS = B * H // 2
NE = 8
THRESHOLD = 0.1
EPS = 1e-5
MAGIC = 12582912.0
CHUNKS = N // 128
RING = 4


def ge(eng, sem, value):
    if isinstance(value, int) and value <= 0:
        return
    eng.wait_ge(sem, value)


def apart(eng, spare):
    eng.sem_inc(spare)


def prologue(nc, x, c, wmod, hT_d, consts):
    ident, modT, gates, cM, spare = (consts[k] for k in ("ident", "modT", "gates", "cM", "spare"))
    with ExitStack() as ctx:
        sb = lambda n, s, d=FP32: ctx.enter_context(nc.sbuf_tensor(n, s, d))
        sem = lambda n: ctx.enter_context(nc.semaphore(n))
        wm = sb("wm", [128, KC, 6 * D])
        cT = sb("cT", [128, KC, B])
        en = sb("en", [128, KC, B])
        silu = sb("silu", [128, KC, B])
        siluB = sb("siluB", [128, KC, B, 128])
        sgn = sb("sgn", [128, 512])
        mag = sb("mag", [128, 512])
        cI = sb("cI", [128, N], I32)
        xt = sb("xt", [128, 8, D])
        st = sb("st", [128, 8, 6])
        mv = sb("mv", [128, 8, 2])
        rs = sb("rs", [128, 8])
        xn = sb("xn", [128, 8, D])
        hT = sb("hTa", [128, KC, N])
        eps = sb("eps", [128, 1])
        pm = ctx.enter_context(nc.psum_tensor("pm", [128, 512], FP32))
        pg = [ctx.enter_context(nc.psum_tensor(f"pg{i}", [128, 512], FP32)) for i in range(2)]
        pt = [ctx.enter_context(nc.psum_tensor(f"pt{i}", [128, 512], FP32)) for i in range(4)]
        loaded = sem("a_loaded")
        x_loaded = sem("a_x_loaded")
        exp_done = sem("a_exp")
        silu_done = sem("a_silu")
        mod_done = sem("a_mod")
        gate_mm = sem("a_gate_mm")
        modT_ready = sem("a_modT")
        chain = sem("a_chain")
        consts_made = sem("a_consts")
        std_done = sem("a_std")
        var_done = sem("a_var")
        norm_done = sem("a_norm")
        tr_done = sem("a_tr")
        h_done = sem("a_h")
        stored = sem("a_stored")
        gate_used = sem("a_gate_used")
        block = ctx.enter_context(nc.Block())

        @block.sync
        def _(sp):
            with nc.allow_non_contiguous_dma("1024 floats of the condition, once"):
                for k in range(KC):
                    sp.dma_start(cT[:, k, :], c[:, k * 128:(k + 1) * 128].rearrange("b p -> p b")).then_inc(loaded, 16)
            sp.dma_start(wm[:, :, :], wmod.rearrange("(k p) n -> p k n", p=128)).then_inc(loaded, 16)
            with sp.Fori(0, B) as b:
                sp.dma_start(xt[:, :, :], x[bass.ds(b, 1)].rearrange("a (t p) d -> p (a t) d", p=128)).then_inc(x_loaded, 16)
                sp.wait_ge(h_done, 4 * b + 4)
                apart(sp, spare)
                sp.dma_start(hT_d[bass.ds(b, 1)].rearrange("a p k n -> p (a k) n"), hT[:, :, :]).then_inc(stored, 16)
                sp.wait_ge(stored, 16 * b + 16)
                apart(sp, spare)

        @block.gpsimd
        def _(gp):
            gp.memset(consts["one"][:, :], 1.0).then_inc(consts_made, 1)
            gp.memset(ident[:, :], 0.0).then_inc(consts_made, 1)
            gp.wait_ge(consts_made, 2)
            gp.affine_select(out=ident[:, :], in_=ident[:, :], compare_op=ALU.not_equal, fill=1.0, base=0,
                             pattern=[[-1, 128]], channel_multiplier=1).then_inc(consts_made, 1)
            gp.iota(cI[:, :], pattern=[[-1, N]], base=N - 1, channel_multiplier=0).then_inc(consts_made, 1)
            gp.wait_ge(consts_made, 4)
            gp.tensor_scalar(cM[:, :], cI[:, :], MAGIC, None, ALU.add).then_inc(consts_made, 1)

        @block.scalar
        def _(act):
            act.wait_ge(loaded, 48)
            act.activation(en[:, :, :], cT[:, :, :], ACT.Exp, scale=-1.0).then_inc(exp_done, 1)
            act.wait_ge(modT_ready, 1)
            with act.Fori(0, B) as b:
                act.wait_ge(var_done, b + 1)
                act.activation(rs[:, :], mv[:, :, 1], ACT.Sqrt, bias=eps[:, 0:1]).then_inc(std_done, 1)
                for i in range(4):
                    k = i // 2
                    act.wait_ge(tr_done, 4 * b + i + 1)
                    apart(act, spare)
                    act.activation(hT[:, k, (i % 2) * 512:(i % 2) * 512 + 512], pt[i][:, :], ACT.Identity,
                                   scale=modT[:, 2 + k, bass.ds(b, 1)], bias=modT[:, k, bass.ds(b, 1)]).then_inc(h_done, 1)

        @block.tensor
        def _(pe):
            pe.wait_ge(silu_done, 1)
            for ch in range(12):
                for k in range(KC):
                    last = pe.matmul(pm[:, ch * B:(ch + 1) * B], wm[:, k, ch * 128:(ch + 1) * 128], silu[:, k, :],
                                     start=(k == 0), stop=(k == KC - 1))
            last.then_inc(mod_done, 1)
            pe.wait_ge(silu_done, 2)
            for b in range(B):
                ge(pe, gate_used, b - 1)
                for i, part in enumerate((2, 5)):
                    for k in range(KC):
                        last = pe.matmul(pg[b % 2][:, i * D:(i + 1) * D], siluB[:, k, b, :],
                                         wm[:, k, part * D:(part + 1) * D], start=(k == 0), stop=(k == KC - 1))
                last.then_inc(gate_mm, 1)
            pe.wait_ge(consts_made, 3)
            with pe.Fori(0, B) as b:
                pe.wait_ge(norm_done, b + 1)
                for i in range(4):
                    k, half = i // 2, i % 2
                    for t in range(4):
                        last = pe.transpose(pt[i][:, t * 128:(t + 1) * 128],
                                            xn[:, half * 4 + t, k * 128:(k + 1) * 128], ident[:, :])
                    last.then_inc(tr_done, 1)

        @block.vector
        def _(dve):
            done = [0]

            def link(ins):
                done[0] += 1
                ins.then_inc(chain, 1)
                dve.wait_ge(chain, done[0])

            link(dve.memset(eps[:, :], EPS))
            dve.wait_ge(exp_done, 1)
            link(dve.tensor_scalar(en[:, :, :], en[:, :, :], 1.0, None, ALU.add))
            link(dve.reciprocal(en[:, :, :], en[:, :, :]))
            dve.tensor_tensor(silu[:, :, :], cT[:, :, :], en[:, :, :], ALU.mult).then_inc(silu_done, 1)
            dve.wait_ge(silu_done, 1)
            dve.tensor_copy(siluB[:, :, :, :], silu[:, :, :].unsqueeze(3).broadcast_to([128, KC, B, 128])).then_inc(silu_done, 1)
            dve.wait_ge(mod_done, 1)
            link(dve.tensor_copy(modT[:, :, :], pm[:, 0:12 * B].rearrange("p (m b) -> p m b", b=B)))
            link(dve.tensor_scalar(modT[:, 2:4, :], modT[:, 2:4, :], 1.0, None, ALU.add))
            dve.tensor_scalar(modT[:, 8:10, :], modT[:, 8:10, :], 1.0, None, ALU.add).then_inc(modT_ready, 1)
            for b in range(B):
                dve.wait_ge(gate_mm, b + 1)
                link(dve.tensor_scalar(sgn[:, :], pg[b % 2][:, :], 0.0, 2.0, ALU.is_ge, ALU.mult))
                link(dve.tensor_scalar(mag[:, :], pg[b % 2][:, :], -1.0, None, ALU.mult))
                link(dve.tensor_tensor(mag[:, :], mag[:, :], pg[b % 2][:, :], ALU.max))
                link(dve.tensor_scalar(mag[:, :], mag[:, :], 0.25, None, ALU.max))
                dve.scalar_tensor_tensor(gates[:, b, :], sgn[:, :], -1.0, mag[:, :], ALU.add, ALU.mult).then_inc(gate_used, 1)
                dve.wait_ge(gate_used, b + 1)
            base = done[0]
            dve.wait_ge(chain, base)
            per = 2
            with dve.Fori(0, B) as b:
                dve.wait_ge(x_loaded, 16 * b + 16)
                for t in range(8):
                    last = dve.bn_stats(st[:, t, :], xt[:, t, :])
                last.then_inc(chain, 1)
                dve.wait_ge(chain, base + per * b + 1)
                apart(dve, spare)
                for t in range(8):
                    last = dve.bn_aggr(mv[:, t, :], st[:, t, :])
                last.then_inc(var_done, 1)
                dve.wait_ge(std_done, b + 1)
                dve.reciprocal(rs[:, :], rs[:, :]).then_inc(chain, 1)
                dve.wait_ge(chain, base + per * b + 2)
                dve.wait_ge(var_done, b + 1)
                for t in range(8):
                    last = dve.tensor_scalar(xn[:, t, :], xt[:, t, :], mv[:, t, 0:1], rs[:, t:t + 1], ALU.subtract, ALU.mult)
                last.then_inc(norm_done, 1)
                dve.wait_ge(norm_done, b + 1)
                dve.wait_ge(tr_done, 4 * b + 4)


def attention(nc, m, blk, hT_d, Wq, Wkv, attnT_d, consts, tag, NB, W, ZW, guard=None):
    ident, cM, posR, minpos, spare = (consts[k] for k in ("ident", "cM", "posR", "minpos", "spare"))
    IW = NB * 128
    UH = N // IW
    UP = 2 * UH
    UB = 2 * UP
    FAR = N - W
    FCH = (N - ZW) // 128
    NEAR = CHUNKS - FCH
    EX = ZW - W
    sem = lambda n: m.sem(f"{tag}_{n}")
    S_ready, S_act, S_max = sem("S_ready"), sem("S_act"), sem("S_max")
    A_ready, A_step = sem("A_ready"), sem("A_step")
    pool_ready, B_step = sem("pool_ready"), sem("B_step")
    far_bias, z_ready = sem("far_bias"), sem("z_ready")
    row_mm, row_set = sem("row_mm"), sem("row_set")
    T_ready, exp_done, pv_done = sem("T_ready"), sem("exp_done"), sem("pv_done")
    C_step, out_ready = sem("C_step"), sem("out_ready")
    stored = [sem("stored_even"), sem("stored_odd")]
    loaded = [sem("loaded_even"), sem("loaded_odd")]
    proj_mm, proj_set, D_ready = sem("proj_mm"), sem("proj_set"), sem("D_ready")
    w_ready, cross_zeroed = sem("w_ready"), sem("cross_zeroed")
    PJ = 8

    def v3(t):
        return t[:, 0:NB * W].rearrange("p (t w) -> p t w", w=W)

    Tb, Q, P = v3(m.Tb), v3(m.Q), v3(m.P)
    fM = v3(m.fM)
    w_, s16, cross, X = ([v3(t) for t in ts] for ts in (m.w, m.s16, m.cross, m.X))
    mk = [v3(t) for t in m.mk]
    zs, zf = ([t[:, 0:NB * ZW].rearrange("p (t w) -> p t w", w=ZW) for t in ts] for ts in (m.zs, m.zf))
    fmax, zmax, nm, nfar, mcol = m.fmax, m.zmax, m.nm, m.nfar, m.mcol

    def place(s):
        return s // UP % 2, s % UP // UH, s % UH

    KA = 4
    KB = 12 + 6 + (3 if FAR else 0)
    nbody = PAIRS // 2

    def load_pair(sp, n, pp):
        ge(sp, proj_mm, PJ * (n - 1))
        apart(sp, spare)
        bi, p = n // (H // 2), n % (H // 2)
        sp.dma_start(m.hTb[pp][:, :, :], hT_d[bass.ds(bi, 1)].rearrange("a p k n -> p (a k) n")).then_inc(loaded[pp], 16)
        for i, (src, off) in enumerate(((Wq, 0), (Wkv, 0), (Wkv, H * DH))):
            sp.dma_start(m.wp[pp][:, :, i, :],
                         src.rearrange("(k p) n -> p k n", p=128)[:, :, bass.ds(p * 128 + off, 128)]).then_inc(loaded[pp], 16)

    def bank_free(pe, rows, uses):
        ge(pe, row_set, rows)
        ge(pe, proj_set, uses)

    def pe_project(pe, n, pp, uses, rows):
        hT, wp = m.hTb[pp], m.wp[pp]
        for i in uses:
            bank_free(pe, rows, PJ * n + i)
            if i < 4:
                for k in range(KC):
                    last = pe.matmul(m.pM[:, :], wp[:, k, i // 2, :], hT[:, k, (i % 2) * 512:(i % 2) * 512 + 512],
                                     start=(k == 0), stop=(k == KC - 1))
            elif i < 6:
                for t in range(4):
                    tok = ((i - 4) * 4 + t) * 128
                    for k in range(KC):
                        last = pe.matmul(m.pM[:, t * 128:(t + 1) * 128], hT[:, k, tok:tok + 128], wp[:, k, 2, :],
                                         start=(k == 0), stop=(k == KC - 1))
            else:
                for t in range(8):
                    last = pe.matmul(m.pM[:, t * PTS:(t + 1) * PTS], m.qa[pp][i - 6][0:DH, t * 128:(t + 1) * 128],
                                     posR[0:DH, :], start=True, stop=True)
            last.then_inc(proj_mm, 1)

    def pe_scores(pe, g, s):
        pp, h, part = place(s)
        for t in range(NB):
            n = g * NB + t
            ge(pe, S_act, n - 1)
            if FAR:
                ge(pe, S_max, n - 1)
            for half in range(2):
                last = pe.matmul(m.pS[(s * NB + t) % 2][:, half * 512:half * 512 + 512],
                                 m.qa[pp][h][0:DH, part * IW + t * 128:part * IW + (t + 1) * 128],
                                 m.ka[pp][h][0:DH, half * 512:half * 512 + 512], start=True, stop=True)
            last.then_inc(S_ready, 1)

    def pe_values(pe, g, s, uses):
        pp, h, part = place(s)
        par = s % 2
        if FCH:
            pe.wait_ge(far_bias, g + 1)
            bank_free(pe, g, uses)
            for t in range(NB):
                last = pe.matmul(m.pM[0:1, t * 128:(t + 1) * 128], nfar[par][:, t:t + 1], ident[:, :], start=True, stop=True)
            last.then_inc(row_mm, 1)
            pe.wait_ge(row_set, g + 1)

        def logits(c):
            n = g * CHUNKS + c
            ge(pe, exp_done, n - 1)
            bank = m.pT[c % 2]
            if c < FCH:
                last = pe.matmul(bank[:, 0:IW], m.ka[pp][h][:, c * 128:(c + 1) * 128],
                                 m.qa[pp][h][:, part * IW:(part + 1) * IW], start=True, stop=True)
            else:
                if c == FCH:
                    pe.wait_ge(z_ready, g + 1)
                for t in range(NB):
                    last = pe.transpose(bank[:, t * 128:(t + 1) * 128],
                                        zf[par][:, t, (c - FCH) * 128:(c - FCH + 1) * 128], ident[:, :])
            last.then_inc(T_ready, 1)

        logits(0)
        logits(1)
        ge(pe, out_ready, g)
        for c in range(CHUNKS):
            pe.wait_ge(exp_done, g * CHUNKS + c + 1)
            pe.matmul(m.pO[:, 0:IW], m.va[pp][:, c, h, :], m.pr[c % RING][:, 0:IW], start=(c == 0),
                      stop=(c == CHUNKS - 1)).then_inc(pv_done, 1)
            if c + 2 < CHUNKS:
                logits(c + 2)

    def act_scores(act, g, s):
        par = s % 2
        ge(act, A_ready, g)
        ge(act, z_ready, g - 1)
        for t in range(NB):
            act.wait_ge(S_ready, g * NB + t + 1)
            sl = m.pS[(s * NB + t) % 2]
            act.activation(Tb[:, t, :], sl[:, FAR:N], ACT.Tanh, scale=0.5)
            act.activation(zs[par][:, t, :], sl[:, N - ZW:N], ACT.Copy).then_inc(S_act, 1)

    def act_project(act, n, pp, uses):
        for i in uses:
            act.wait_ge(proj_mm, PJ * n + i + 1)
            cols = slice((i % 2) * 512, (i % 2) * 512 + 512)
            if i < 4:
                dst = (m.qa if i < 2 else m.ka)[pp]
                scale = DH ** -0.5 if i < 2 else 1.0
                act.activation(dst[0][0:DH, cols], m.pM[0:DH, :], ACT.Copy, scale=scale)
                last = act.activation(dst[1][0:DH, cols], m.pM[DH:128, :], ACT.Copy, scale=scale)
            elif i < 6:
                t = (i - 4) * 4
                last = act.activation(m.va[pp][:, t:t + 4, :, 0:DH],
                                      m.pM[:, :].rearrange("p (t h d) -> p t h d", t=4, h=2), ACT.Copy)
            else:
                last = act.activation(m.ER[pp][i - 6][:, :, :], m.pM[:, :].rearrange("p (t d) -> p t d", t=8), ACT.Copy)
            last.then_inc(proj_set, 1)

    def act_values(act, g, s):
        pp, h, part = place(s)
        if FCH:
            act.wait_ge(row_mm, g + 1)
            act.activation(m.qa[pp][h][DH:DH + 1, part * IW:(part + 1) * IW], m.pM[0:1, 0:IW], ACT.Copy).then_inc(row_set, 1)
        for c in range(CHUNKS):
            n = g * CHUNKS + c
            act.wait_ge(T_ready, n + 1)
            ge(act, pv_done, n + 1 - RING)
            act.activation(m.pr[c % RING][:, 0:IW], m.pT[c % 2][:, 0:IW], ACT.Exp).then_inc(exp_done, 1)

    def pool_tables(gp, n, pp):
        for h in range(2):
            gp.wait_ge(proj_set, PJ * n + 7 + h)
            gp.tensor_tensor(m.DR[pp][h][:, :, 1:PTS], m.ER[pp][h][:, :, 0:PTS - 1], m.ER[pp][h][:, :, 1:PTS],
                             ALU.subtract).then_inc(D_ready, 1)

    def pool_unit(gp, g, s, n):
        pp, h, part = place(s)
        par = s % 2
        gp.wait_ge(A_ready, g + 1)
        ge(gp, z_ready, g - 1)
        gp.tensor_tensor(cross[par][:, :, 0:W - 1], fM[:, :, 0:W - 1], fM[:, :, 1:W], ALU.subtract).then_inc(pool_ready, 1)
        gp.wait_ge(D_ready, 2 * n + h + 1)
        apart(gp, spare)
        for t in range(NB):
            last = gp.tensor_copy(X[par][:, t, :].rearrange("p (r u) -> p r u", u=PTS),
                                  m.DR[pp][h][:, part * NB + t, :].unsqueeze(1).broadcast_to([128, W // PTS, PTS]))
        last.then_inc(pool_ready, 1)

    def dve_positions(dve, g, s):
        par = s % 2
        ge(dve, w_ready, g)
        for t in range(NB):
            dve.wait_ge(S_ready, g * NB + t + 1)
            sl = m.pS[(s * NB + t) % 2]
            if FAR:
                dve.reduce_max(fmax[par][:, t:t + 1], sl[:, 0:512], AX)
            dve.wait_ge(S_act, g * NB + t + 1)
            if FAR:
                dve.reduce_max(fmax[par][:, NB + t:NB + t + 1], sl[:, 512:FAR], AX).then_inc(S_max, 1)
            last = dve.tensor_tensor_scan(Q[:, t, ::-1], Tb[:, t, ::-1], m.one[:, 0:1].broadcast_to([128, W]), 0.0,
                                          ALU.add, ALU.add)
        last.then_inc(A_step, 1)
        dve.wait_ge(A_step, KA * g + 1)
        dve.tensor_scalar(P, Q, 0.5, CAP, ALU.mult, ALU.min).then_inc(A_step, 1)
        dve.wait_ge(A_step, KA * g + 2)
        dve.tensor_scalar(Q, P, 0.5, MAGIC, ALU.subtract, ALU.add).then_inc(A_step, 1)
        dve.tensor_tensor(minpos[:, 0:NB], minpos[:, 0:NB], P[:, :, 0], ALU.min).then_inc(A_step, 1)
        dve.wait_ge(A_step, KA * g + 4)
        ge(dve, pool_ready, 2 * g)
        for t in range(NB):
            last = dve.tensor_tensor_scan(fM[:, t, ::-1], m.one[:, 0:1].broadcast_to([128, W]), Q[:, t, ::-1],
                                          MAGIC - 1.0, ALU.add, ALU.min)
        last.then_inc(A_ready, 1)
        dve.wait_ge(A_ready, g + 1)
        dve.tensor_tensor(s16[par], cM[:, N - W:N].unsqueeze(1).broadcast_to([128, NB, W]), fM, ALU.subtract)
        dve.scalar_tensor_tensor(w_[par], fM, MAGIC, P, ALU.subtract, ALU.subtract, reverse1=True).then_inc(w_ready, 1)

    def dve_logits(dve, g, s):
        pp, h, part = place(s)
        par = s % 2
        x = X[par]
        step = [0]

        def link(ins, alone=False):
            step[0] += 1
            ins.then_inc(B_step, 1)
            dve.wait_ge(B_step, KB * g + step[0])
            if alone:
                apart(dve, spare)

        dve.wait_ge(pool_ready, 2 * g + 2)
        dve.wait_ge(w_ready, g + 1)
        ge(dve, cross_zeroed, 2)
        for bit in (5, 4, 3, 2, 1, 0):
            sh = 1 << bit
            link(dve.tensor_scalar(mk[bit % 2], s16[par], sh, None, ALU.bitwise_and), alone=True)
            link(dve.copy_predicated(x[:, :, 0:W - sh], mk[bit % 2][:, :, 0:W - sh], x[:, :, sh:W]))
        cr = cross[par]
        link(dve.tensor_tensor(cr[:, :, 0:W - 1], cr[:, :, 0:W - 1], x[:, :, 1:W], ALU.mult))
        for t in range(NB):
            last = dve.tensor_tensor_scan(Q[:, t, ::-1], m.one[:, 0:1].broadcast_to([128, W]), cr[:, t, ::-1],
                                          m.ER[pp][h][:, part * NB + t, PTS - 1:PTS], ALU.mult, ALU.add)
        last.then_inc(B_step, 1)
        dve.tensor_tensor(x, w_[par], x, ALU.mult).then_inc(B_step, 1)
        step[0] += 2
        dve.wait_ge(B_step, KB * g + step[0])
        link(dve.tensor_tensor(x, x, Q, ALU.add))
        z = zs[par]
        dve.wait_ge(S_act, (g + 1) * NB)
        link(dve.tensor_tensor(z[:, :, EX:ZW], z[:, :, EX:ZW], x, ALU.add))
        link(dve.tensor_reduce(zmax[:, 0:NB], z[:, :, EX:ZW], AX, ALU.max))
        if FAR:
            last_entry = m.ER[pp][h][:, part * NB:(part + 1) * NB, 0]
            link(dve.tensor_tensor(mcol[:, 0:NB], fmax[par][:, 0:NB], fmax[par][:, NB:2 * NB], ALU.max))
            link(dve.tensor_tensor(mcol[:, 0:NB], mcol[:, 0:NB], last_entry, ALU.add))
            link(dve.tensor_tensor(mcol[:, 0:NB], mcol[:, 0:NB], zmax[:, 0:NB], ALU.max))
            ge(dve, row_mm, g - 1)
            dve.tensor_tensor(nfar[par][:, 0:NB], last_entry, mcol[:, 0:NB], ALU.subtract).then_inc(far_bias, 1)
            dve.wait_ge(far_bias, g + 1)
            top = mcol
        else:
            top = zmax
        ge(dve, T_ready, (g - 1) * CHUNKS)
        for t in range(NB):
            if EX:
                dve.tensor_scalar(zf[par][:, t, 0:EX], z[:, t, 0:EX], nfar[par][:, t:t + 1], None, ALU.add)
            last = dve.tensor_scalar(zf[par][:, t, EX:ZW], z[:, t, EX:ZW], top[:, t:t + 1], None, ALU.subtract)
        last.then_inc(z_ready, 1)
        dve.wait_ge(z_ready, g + 1)
        assert step[0] == KB, (step[0], KB)

    def dve_out(dve, g, s):
        par = s % 2
        dve.wait_ge(pv_done, (g + 1) * CHUNKS)
        dve.reciprocal(m.rc[:, 0:IW], m.pO[DH:128, 0:IW]).then_inc(C_step, 1)
        dve.wait_ge(C_step, g + 1)
        ge(dve, stored[par], 16 * (g // 2))
        dve.tensor_tensor(m.oT[par][:, 0:IW], m.pO[0:DH, 0:IW], m.rc[:, 0:IW], ALU.mult).then_inc(out_ready, 1)
        dve.wait_ge(out_ready, g + 1)

    def body(eng_slot, it):
        for s in range(UB):
            eng_slot(it, s, it * UB + s)

    def run(eng, slot):
        body(slot, 0)
        with eng.Fori(1, nbody - 1) as it:
            body(slot, it)
        body(slot, nbody - 1)

    def older(it, s, g, back):
        if isinstance(it, int) and it * UB + s < back:
            return None
        return g - back, (s - back) % UB

    def project_at(it, s):
        pp, off = s // UP, s % UP
        if off not in (2, 3):
            return None
        if isinstance(it, int) and it == nbody - 1 and pp == 1:
            return None
        return 2 * it + pp + 1, (pp + 1) % 2, (0, 1, 2, 3) if off == 2 else (4, 5, 6, 7)

    def pe_all(pe):
        pe.wait_ge(loaded[0], 64)
        pe_project(pe, 0, 0, range(PJ), 0)

        def slot(it, s, g):
            pe_scores(pe, g, s)
            done_uses = PJ * (2 * it + s // UP + 1) + (0 if s % UP < 3 else 4 if s % UP == 3 else 8)
            if isinstance(it, int) and it == nbody - 1 and s // UP == 1:
                done_uses = PJ * PAIRS
            old = older(it, s, g, 2)
            if old:
                pe_values(pe, *old, done_uses)
            pj = project_at(it, s)
            if pj:
                n, pp, which = pj
                if which[0] == 0:
                    pe.wait_ge(loaded[pp], 64 * (it + 2 - pp))
                pe_project(pe, n, pp, which, (g - 1) if FCH else 0)
        run(pe, slot)
        for back in (2, 1):
            g = nbody * UB - back
            pe_values(pe, g, g % UB, PJ * PAIRS)

    def act_all(act):
        act_project(act, 0, 0, range(PJ))

        def slot(it, s, g):
            act_scores(act, g, s)
            old = older(it, s, g, 2)
            if old:
                act_values(act, *old)
            pj = project_at(it, s)
            if pj:
                act_project(act, *pj)
        run(act, slot)
        for back in (2, 1):
            g = nbody * UB - back
            act_values(act, g, g % UB)

    def pool_all(gp):
        for par in range(2):
            gp.memset(cross[par][:, :, W - 1:W], 0.0).then_inc(cross_zeroed, 1)
        pool_tables(gp, 0, 0)

        def slot(it, s, g):
            pool_unit(gp, g, s, 2 * it + s // UP)
            pj = project_at(it, s)
            if pj and pj[2][0] == 4:
                pool_tables(gp, pj[0], pj[1])
        run(gp, slot)

    def dve_all(dve):
        def slot(it, s, g):
            dve_positions(dve, g, s)
            old = older(it, s, g, 3)
            if old:
                dve_out(dve, *old)
            old = older(it, s, g, 1)
            if old:
                dve_logits(dve, *old)
        run(dve, slot)
        G = nbody * UB
        dve_out(dve, G - 3, (G - 3) % UB)
        dve_logits(dve, G - 1, (G - 1) % UB)
        dve_out(dve, G - 2, (G - 2) % UB)
        dve_out(dve, G - 1, (G - 1) % UB)

    def sp_store(sp, it, s, g):
        pp, h, part = place(s)
        sp.wait_ge(out_ready, g + 1)
        apart(sp, spare)
        n = 2 * it + pp
        sp.dma_start(attnT_d[bass.ds(n, 1), h, :, part * IW:(part + 1) * IW].rearrange("a d n -> (a d) n"),
                     m.oT[s % 2][:, 0:IW]).then_inc(stored[s % 2], 16)

    def sp_all(sp):
        load_pair(sp, 0, 0)
        load_pair(sp, 1, 1)

        def one(it):
            for s in range(UB):
                sp_store(sp, it, s, it * UB + s)
                if s % UP == 0 and not (isinstance(it, int) and it == nbody - 1):
                    load_pair(sp, 2 * it + 2 + s // UP, s // UP)
        one(0)
        with sp.Fori(1, nbody - 1) as it:
            one(it)
        one(nbody - 1)
        for par in range(2):
            sp.wait_ge(stored[par], 16 * nbody * UB // 2)

    def guarded(eng, work):
        if guard is None:
            work(eng)
        else:
            need = eng.value_load(guard[0:1, 0:1], min_val=0, max_val=128)
            with eng.If(need != 0):
                work(eng)

    @blk.sync
    def _(sp):
        guarded(sp, sp_all)

    @blk.tensor
    def _(pe):
        guarded(pe, pe_all)

    @blk.scalar
    def _(act):
        guarded(act, act_all)

    @blk.gpsimd
    def _(gp):
        guarded(gp, pool_all)

    @blk.vector
    def _(dve):
        guarded(dve, dve_all)


def coverage(nc, m, consts, flag):
    with ExitStack() as ctx:
        minpos, low, low1, ps = consts["minpos"], m.zmax, m.mcol[:, 0:1], m.pM
        compared = ctx.enter_context(nc.semaphore("f_compared"))
        counted = ctx.enter_context(nc.semaphore("f_counted"))
        flagged = ctx.enter_context(nc.semaphore("f_flagged"))
        block = ctx.enter_context(nc.Block())

        @block.vector
        def _(dve):
            dve.tensor_scalar(low[:, :], minpos[:, :], CAP, None, ALU.is_lt).then_inc(compared, 1)
            dve.wait_ge(compared, 1)
            dve.reduce_max(low1, low[:, :], AX).then_inc(compared, 1)
            dve.wait_ge(counted, 1)
            dve.tensor_copy(flag[0:1, 0:1], ps[0:1, 0:1]).then_inc(flagged, 1)
            dve.wait_ge(flagged, 1)

        @block.tensor
        def _(pe):
            pe.wait_ge(compared, 2)
            pe.matmul(ps[0:1, 0:1], low1, consts["one"][:, :], start=True, stop=True).then_inc(counted, 1)


def feed_forward(nc, x, attnT_d, weights, consts, out):
    Wout, b_out, gate_w, gate_b, expert_w, expert_b = weights
    ident, modT, gates, spare = (consts[k] for k in ("ident", "modT", "gates", "spare"))
    NT = TOK // 128
    with ExitStack() as ctx:
        sb = lambda n, s, d=FP32: ctx.enter_context(nc.sbuf_tensor(n, s, d))
        sem = lambda n: ctx.enter_context(nc.semaphore(n))
        pb = lambda n: ctx.enter_context(nc.psum_tensor(n, [128, 512], FP32))
        wo = sb("wo", [128, H * DH // 128, D])
        ew = sb("ew", [128, KC, NE, D])
        gw = sb("gw", [128, KC, NE])
        bo = sb("bo", [128, D])
        gb = sb("gb", [128, NE])
        eb = sb("eb", [NE, D])
        aT = [sb(f"aT{i}", [128, H * DH // 128, 128]) for i in range(2)]
        xt = [sb(f"xr{i}", [128, D]) for i in range(2)]
        x1 = [sb(f"x1_{i}", [128, D]) for i in range(2)]
        y = sb("y", [128, D])
        st = sb("st2", [128, 6])
        mv = sb("mv2", [128, 2])
        sd = sb("sd", [128, 1])
        rstd = sb("rstd", [128, 1])
        xn = sb("xn2", [128, D])
        eps = sb("eps2", [128, 1])
        h2T = [sb(f"h2T{i}", [128, KC, 128]) for i in range(2)]
        lg = sb("lg", [128, NE])
        mx = sb("mx", [128, 1])
        ex = sb("ex", [128, NE])
        sm = sb("sm", [128, 1])
        rsm = sb("rsm", [128, 1])
        pr = sb("prg", [128, NE])
        sel = sb("sel", [128, NE])
        ws = sb("ws", [128, 1])
        z0 = sb("z0", [128, 1])
        rws = sb("rws", [128, 1])
        wgt = sb("wgt", [128, NE])
        wT = sb("wT", [NE, 128])
        acc = sb("acc", [128, D])
        res = [sb(f"res{i}", [128, D]) for i in range(2)]
        pY, pH, pG, pB = pb("pY"), pb("pH"), pb("pG"), pb("pB")
        pE = [pb(f"pE{i}") for i in range(4)]
        w_loaded = sem("p_w_loaded")
        in_loaded = [sem("p_in_even"), sem("p_in_odd")]
        y_mm, y_used, x1_made = sem("p_y_mm"), sem("p_y_used"), sem("p_x1")
        chain = sem("p_chain")
        var_done, std_done, norm_done = sem("p_var"), sem("p_std"), sem("p_norm")
        tr_mm, h_set = sem("p_tr"), sem("p_h")
        gate_mm, ex_in, ex_out = sem("p_gate"), sem("p_ex_in"), sem("p_ex_out")
        exp_mm, exp_used = sem("p_experts"), sem("p_experts_used")
        w_made, wT_mm, wT_set, bias_mm, acc_done = sem("p_w"), sem("p_wT"), sem("p_wTs"), sem("p_bias"), sem("p_acc")
        stored = [sem("p_stored_even"), sem("p_stored_odd")]
        eps_set = sem("p_eps")
        block = ctx.enter_context(nc.Block())
        K1, K2 = 3, 15

        def run(eng, slot):
            for s in range(2):
                slot(0, s, s)
            with eng.Fori(1, NT // 2) as it:
                for s in range(2):
                    slot(it, s, 2 * it + s)

        def tile_before(it, s):
            return not (isinstance(it, int) and it == 0 and s == 0)

        def batch_gate(i, part):
            return gates[:, bass.ds(i // (N // 128), 1), part * D:(part + 1) * D].rearrange("p a d -> p (a d)")

        @block.sync
        def _(sp):
            sp.dma_start(wo[:, :, :], Wout.rearrange("(k p) n -> p k n", p=128)).then_inc(w_loaded, 16)
            for e in range(NE):
                sp.dma_start(ew[:, :, e, :], expert_w[e].rearrange("(k p) n -> p k n", p=128)).then_inc(w_loaded, 16)
            with nc.allow_non_contiguous_dma("small weights, once"):
                sp.dma_start(gw[:, :, :], gate_w.rearrange("(k p) n -> p k n", p=128)).then_inc(w_loaded, 16)
                sp.dma_start(bo[:, :], b_out.rearrange("(a n) -> a n", a=1).broadcast_to([128, D])).then_inc(w_loaded, 16)
                sp.dma_start(gb[:, :], gate_b.rearrange("(a n) -> a n", a=1).broadcast_to([128, NE])).then_inc(w_loaded, 16)
                sp.dma_start(eb[:, :], expert_b).then_inc(w_loaded, 16)

            def load(i, par):
                bi, t = i // (N // 128), i % (N // 128)
                ge(sp, x1_made, i - 1)
                apart(sp, spare)
                sp.dma_start(xt[par][:, :], x.rearrange("b n d -> (b n) d")[bass.ds(i * 128, 128), :]).then_inc(in_loaded[par], 16)
                sp.dma_start(aT[par][:, :, :],
                             attnT_d.rearrange("(b k) h d n -> b (h d) k n", b=B)[
                                 bass.ds(bi, 1), :, :, bass.ds(t * 128, 128)].rearrange("a p k n -> p (a k) n")
                             ).then_inc(in_loaded[par], 16)

            def store(i, par):
                sp.wait_ge(acc_done, i + 1)
                apart(sp, spare)
                sp.dma_start(out.rearrange("b n d -> (b n) d")[bass.ds(i * 128, 128), :], res[par][:, :]).then_inc(stored[par], 16)

            def slot(it, s, i):
                load(i, s)
                if tile_before(it, s):
                    store(i - 1, 1 - s)
            run(sp, slot)
            store(NT - 1, 1)
            for par in range(2):
                sp.wait_ge(stored[par], 16 * NT // 2)

        @block.tensor
        def _(pe):
            pe.wait_ge(w_loaded, 16 * (NE + 5))

            def stage1(it, s, i):
                pe.wait_ge(in_loaded[s], 32 * (it + 1))
                ge(pe, y_used, i)
                for k in range(H * DH // 128):
                    last = pe.matmul(pY[:, 0:D], aT[s][:, k, :], wo[:, k, :], start=(k == 0), stop=(k == H * DH // 128 - 1))
                last.then_inc(y_mm, 1)

            def experts(i, s):
                h = h2T[s]
                pe.wait_ge(h_set, i + 1)
                ge(pe, wT_set, i)
                for k in range(KC):
                    last = pe.matmul(pG[:, 0:NE], h[:, k, :], gw[:, k, :], start=(k == 0), stop=(k == KC - 1))
                last.then_inc(gate_mm, 1)
                for q in range(4):
                    ge(pe, exp_used, 4 * (i - 1) + q + 1 if isinstance(i, int) else 4 * i + (q - 3))
                    for k in range(KC):
                        last = pe.matmul(pE[q][:, :], h[:, k, :], ew[:, k, 2 * q:2 * q + 2, :].rearrange("p e n -> p (e n)"),
                                         start=(k == 0), stop=(k == KC - 1))
                    last.then_inc(exp_mm, 1)

            def transposes(i):
                pe.wait_ge(norm_done, i + 1)
                ge(pe, h_set, i)
                for k in range(KC):
                    last = pe.transpose(pH[:, k * 128:(k + 1) * 128], xn[:, k * 128:(k + 1) * 128], ident[:, :])
                last.then_inc(tr_mm, 1)

            def biases(i):
                pe.wait_ge(w_made, i + 1)
                pe.transpose(pG[0:NE, 128:256], wgt[:, :], ident[:, :]).then_inc(wT_mm, 1)
                pe.wait_ge(wT_set, i + 1)
                ge(pe, acc_done, i)
                pe.matmul(pB[:, 0:D], wT[:, :], eb[:, :], start=True, stop=True).then_inc(bias_mm, 1)

            def slot(it, s, i):
                stage1(it, s, i)
                if tile_before(it, s):
                    experts(i - 1, 1 - s)
                transposes(i)
                if tile_before(it, s):
                    biases(i - 1)
            run(pe, slot)
            experts(NT - 1, 1)
            biases(NT - 1)

        @block.scalar
        def _(act):
            def stage1(i, s):
                act.wait_ge(var_done, i + 1)
                act.activation(sd[:, :], mv[:, 1:2], ACT.Sqrt, bias=eps[:, 0:1]).then_inc(std_done, 1)

            def turned(i, s):
                act.wait_ge(tr_mm, i + 1)
                ge(act, exp_mm, 4 * (i - 1))
                apart(act, spare)
                bi = i // (N // 128)
                for k in range(KC):
                    last = act.activation(h2T[s][:, k, :], pH[:, k * 128:(k + 1) * 128], ACT.Identity,
                                          scale=modT[:, 8 + k, bass.ds(bi, 1)], bias=modT[:, 6 + k, bass.ds(bi, 1)])
                last.then_inc(h_set, 1)

            def stage2(i):
                act.wait_ge(ex_in, i + 1)
                act.activation(ex[:, :], lg[:, :], ACT.Exp, accum_out=sm[:, :]).then_inc(ex_out, 1)
                act.wait_ge(wT_mm, i + 1)
                ge(act, bias_mm, i)
                act.activation(wT[:, :], pG[0:NE, 128:256], ACT.Copy).then_inc(wT_set, 1)

            act.wait_ge(eps_set, 1)

            def slot(it, s, i):
                stage1(i, s)
                turned(i, s)
                if tile_before(it, s):
                    stage2(i - 1)
            run(act, slot)
            stage2(NT - 1)

        @block.vector
        def _(dve):
            dve.memset(eps[:, :], EPS).then_inc(eps_set, 1)
            dve.wait_ge(w_loaded, 16 * (NE + 5))

            def stage1(it, s, i):
                step = [0]

                def link(ins):
                    step[0] += 1
                    ins.then_inc(chain, 1)
                    dve.wait_ge(chain, K1 * i + K2 * (i - 1 if tile_before(it, s) else 0) + step[0])

                dve.wait_ge(in_loaded[s], 32 * (it + 1))
                dve.wait_ge(y_mm, i + 1)
                dve.tensor_tensor(y[:, :], pY[:, 0:D], bo[:, :], ALU.add).then_inc(y_used, 1)
                dve.wait_ge(y_used, i + 1)
                link(dve.tensor_tensor(y[:, :], y[:, :], batch_gate(i, 0), ALU.mult))
                dve.tensor_tensor(x1[s][:, :], y[:, :], xt[s][:, :], ALU.add).then_inc(x1_made, 1)
                dve.wait_ge(x1_made, i + 1)
                link(dve.bn_stats(st[:, :], x1[s][:, :]))
                ge(dve, std_done, i)
                apart(dve, spare)
                dve.bn_aggr(mv[:, :], st[:, :]).then_inc(var_done, 1)
                dve.wait_ge(std_done, i + 1)
                link(dve.reciprocal(rstd[:, :], sd[:, :]))
                ge(dve, tr_mm, i)
                dve.wait_ge(var_done, i + 1)
                dve.tensor_scalar(xn[:, :], x1[s][:, :], mv[:, 0:1], rstd[:, 0:1], ALU.subtract, ALU.mult).then_inc(norm_done, 1)
                dve.wait_ge(norm_done, i + 1)
                assert step[0] == K1

            def stage2(i, s):
                step = [0]

                def link(ins):
                    step[0] += 1
                    ins.then_inc(chain, 1)
                    dve.wait_ge(chain, K1 * (NT if isinstance(i, int) and i == NT - 1 else i + 2) + K2 * i + step[0])

                dve.wait_ge(gate_mm, i + 1)
                link(dve.tensor_tensor(lg[:, :], pG[:, 0:NE], gb[:, :], ALU.add))
                link(dve.reduce_max(mx[:, :], lg[:, :], AX))
                dve.tensor_scalar(lg[:, :], lg[:, :], mx[:, 0:1], None, ALU.subtract).then_inc(ex_in, 1)
                dve.wait_ge(ex_out, i + 1)
                link(dve.reciprocal(rsm[:, :], sm[:, :]))
                link(dve.tensor_scalar(pr[:, :], ex[:, :], rsm[:, 0:1], None, ALU.mult))
                link(dve.scalar_tensor_tensor(sel[:, :], pr[:, :], THRESHOLD, pr[:, :], ALU.is_ge, ALU.mult))
                link(dve.reduce_sum(ws[:, :], sel[:, :], AX))
                link(dve.tensor_scalar(z0[:, :], ws[:, :], 0.0, None, ALU.is_equal))
                link(dve.tensor_tensor(ws[:, :], ws[:, :], z0[:, :], ALU.add))
                link(dve.reciprocal(rws[:, :], ws[:, :]))
                ge(dve, wT_mm, i)
                dve.tensor_scalar(wgt[:, :], sel[:, :], rws[:, 0:1], None, ALU.mult).then_inc(w_made, 1)
                dve.wait_ge(w_made, i + 1)
                for e in range(NE):
                    if e % 2 == 0:
                        dve.wait_ge(exp_mm, 4 * i + e // 2 + 1)
                    src = pE[e // 2][:, (e % 2) * D:(e % 2 + 1) * D]
                    if e == 0:
                        link(dve.tensor_scalar(acc[:, :], src, wgt[:, 0:1], None, ALU.mult))
                    elif e % 2 == 0:
                        link(dve.scalar_tensor_tensor(acc[:, :], src, wgt[:, e:e + 1], acc[:, :], ALU.mult, ALU.add))
                    else:
                        dve.scalar_tensor_tensor(acc[:, :], src, wgt[:, e:e + 1], acc[:, :], ALU.mult, ALU.add).then_inc(exp_used, 1)
                        dve.wait_ge(exp_used, 4 * i + e // 2 + 1)
                dve.wait_ge(bias_mm, i + 1)
                link(dve.tensor_tensor(acc[:, :], acc[:, :], pB[:, 0:D], ALU.add))
                link(dve.tensor_tensor(acc[:, :], acc[:, :], batch_gate(i, 1), ALU.mult))
                ge(dve, stored[s], 16 * (i // 2))
                dve.tensor_tensor(res[s][:, :], acc[:, :], x1[s][:, :], ALU.add).then_inc(acc_done, 1)
                dve.wait_ge(acc_done, i + 1)
                assert step[0] == K2, step[0]

            def slot(it, s, i):
                stage1(it, s, i)
                if tile_before(it, s):
                    stage2(i - 1, 1 - s)
            run(dve, slot)
            stage2(NT - 1, 1)


class Buffers:

    def __init__(self, nc, ctx):
        sb = lambda n, s, d=FP32: ctx.enter_context(nc.sbuf_tensor(n, s, d))
        pb = lambda n, w=512: ctx.enter_context(nc.psum_tensor(n, [128, w], FP32))
        two = lambda n, s, d=FP32: [sb(f"{n}{i}", s, d) for i in range(2)]
        self.sem = lambda n: ctx.enter_context(nc.semaphore(n))
        self.hTb = two("hTb", [128, KC, N])
        self.wp = two("wp", [128, KC, 3, 128])
        self.qa = [two(f"qa{p}", [DH + 1, N]) for p in range(2)]
        self.ka = [two(f"ka{p}", [DH + 1, N]) for p in range(2)]
        self.va = two("va", [128, CHUNKS, 2, 128])
        self.ER = [two(f"ER{p}", [128, CHUNKS, PTS]) for p in range(2)]
        self.DR = [two(f"DR{p}", [128, CHUNKS, PTS]) for p in range(2)]
        self.Tb, self.Q, self.P, self.fM = (sb(n, [128, N]) for n in ("Tb", "Q", "P", "fM"))
        self.w, self.cross, self.X = two("w", [128, N]), two("cross", [128, N]), two("X", [128, N])
        self.s16, self.mk = two("s16", [128, N], I16), two("mk", [128, N], I16)
        self.zs, self.zf = two("zs", [128, N]), two("zf", [128, N])
        self.fmax, self.nfar = two("fmax", [128, 8]), two("nfar", [128, 8])
        self.zmax, self.mcol = sb("zmax", [128, 8]), sb("mcol", [128, 8])
        self.nm = None
        self.pr = [sb(f"pr{i}", [128, 512]) for i in range(RING)]
        self.rc, self.oT = sb("rc", [DH, 512]), two("oT", [DH, 512])
        self.pS, self.pT = [pb(f"pS{i}", N) for i in range(2)], [pb(f"pT{i}") for i in range(2)]
        self.pO, self.pM = pb("pO"), pb("pM")


def fill(nc, m, pos_emb, consts):
    with ExitStack() as ctx:
        pos = ctx.enter_context(nc.sbuf_tensor("pos", [DH, PTS], FP32))
        loaded = ctx.enter_context(nc.semaphore("i_loaded"))
        filled = ctx.enter_context(nc.semaphore("i_filled"))
        block = ctx.enter_context(nc.Block())

        @block.sync
        def _(sp):
            sp.dma_start(pos[:, :], pos_emb).then_inc(loaded, 16)
            sp.wait_ge(loaded, 16)

        @block.vector
        def _(dve):
            dve.memset(consts["minpos"][:, :], CAP + 1.0).then_inc(filled, 1)
            dve.wait_ge(loaded, 16)
            dve.tensor_scalar(consts["posR"][:, :], pos[:, ::-1], float(DH) ** 0.5, None, ALU.mult).then_inc(filled, 1)
            for p in range(2):
                dve.memset(m.va[p][:, :, :, DH:128], 1.0).then_inc(filled, 1)
                for h in range(2):
                    dve.memset(m.ka[p][h][DH:DH + 1, :], 1.0).then_inc(filled, 1)
                    dve.memset(m.DR[p][h][:, :, 0:1], 0.0).then_inc(filled, 1)
            dve.wait_ge(filled, 12)


def adaln_block(nc, L0_attn_x, L0_attn_Wq, L0_attn_Wkv, L0_attn_Wout, L0_attn_b_out, L0_attn_pos_emb, L0_ffn_gate_w,
                L0_ffn_gate_b, L0_ffn_expert_w, L0_ffn_expert_b, L0_c, L0_wmod, out):
    with ExitStack() as ctx:
        sb = lambda n, s, d=FP32: ctx.enter_context(nc.sbuf_tensor(n, s, d))
        consts = {
            "ident": sb("ident", [128, 128]), "one": sb("one", [128, 1]), "cM": sb("cM", [128, N]),
            "modT": sb("modT", [128, 12, B]), "gates": sb("gates", [128, B, 2 * D]),
            "posR": sb("posR", [DH, PTS]), "minpos": sb("minpos", [128, 8]),
            "spare": ctx.enter_context(nc.semaphore("spare")),
        }
        flag = sb("flag", [1, 2], I32)
        hT_d = nc.dram_tensor("hT_scratch", [B, 128, KC, N], FP32).ap()
        attnT_d = nc.dram_tensor("attnT_scratch", [PAIRS, 2, DH, N], FP32).ap()
        prologue(nc, L0_attn_x, L0_c, L0_wmod, hT_d, consts)
        with ExitStack() as inner:
            m = Buffers(nc, inner)
            m.one = consts["one"]
            fill(nc, m, L0_attn_pos_emb, consts)
            with nc.Block() as near:
                attention(nc, m, near, hT_d, L0_attn_Wq, L0_attn_Wkv, attnT_d, consts, "near", NB=4, W=192, ZW=256)
            coverage(nc, m, consts, flag)
            with nc.Block() as whole:
                attention(nc, m, whole, hT_d, L0_attn_Wq, L0_attn_Wkv, attnT_d, consts, "all", NB=1, W=N, ZW=N, guard=flag)
        feed_forward(nc, L0_attn_x, attnT_d, (L0_attn_Wout, L0_attn_b_out, L0_ffn_gate_w, L0_ffn_gate_b,
                                              L0_ffn_expert_w, L0_ffn_expert_b), consts, out)


_INS = ['L0_attn_x', 'L0_attn_Wq', 'L0_attn_Wkv', 'L0_attn_Wout', 'L0_attn_b_out', 'L0_attn_pos_emb', 'L0_ffn_gate_w',
        'L0_ffn_gate_b', 'L0_ffn_expert_w', 'L0_ffn_expert_b', 'L0_c', 'L0_wmod']
_OUTS = [((4, 1024, 256), 'float32')]


def kernel(**inputs):
    import numpy as _np
    import concourse.bacc as _bacc
    from concourse import mybir as _mybir
    from concourse.bass_utils import run_bass_kernel_spmd as _run

    nc = _bacc.Bacc("TRN2", target_bir_lowering=False, num_devices=1)
    arrays, args = {}, []
    for name in _INS:
        a = _np.ascontiguousarray(inputs[name])
        arrays[f"in_{name}_dram"] = a
        args.append(nc.dram_tensor(f"in_{name}_dram", a.shape, _mybir.dt.from_np(a.dtype), kind="ExternalInput").ap())
    for i, (shape, dtype) in enumerate(_OUTS):
        dt = _mybir.dt.from_np(_np.dtype(dtype))
        args.append(nc.dram_tensor(f"out_{i}_dram", shape, dt, kind="ExternalOutput").ap())
    adaln_block(nc, *args)
    r = _run(nc, [arrays], core_ids=[0])
    return r.results[0]["out_0_dram"]
```

```python
import concourse.bass as bass
from concourse import mybir
from contextlib import ExitStack

FP32 = mybir.dt.float32
F32R = mybir.dt.float32r
I16 = mybir.dt.int16
I32 = mybir.dt.int32
ALU = mybir.AluOpType
ACT = mybir.ActivationFunctionType
AX = mybir.AxisListType.X

B, N, D = 4, 1024, 256
H, DH = 16, 64
PTS = 64
CAP = float(PTS - 1)
KC = D // 128
TOK = B * N
PAIRS = B * H // 2
NE = 8
THRESHOLD = 0.1
EPS = 1e-5
LOWEST = -3.0e38
MAGIC = 12582912.0
CHUNKS = N // 128
RING = 4


def ge(eng, sem, value):
    if isinstance(value, int) and value <= 0:
        return
    eng.wait_ge(sem, value)


def apart(eng, spare):
    eng.sem_inc(spare)


def prologue(nc, x, c, wmod, hT_d, gates_d, consts):
    ident, modT, cM, spare = (consts[k] for k in ("ident", "modT", "cM", "spare"))
    with ExitStack() as ctx:
        sb = lambda n, s, d=FP32: ctx.enter_context(nc.sbuf_tensor(n, s, d))
        sem = lambda n: ctx.enter_context(nc.semaphore(n))
        wm = sb("wm", [128, KC, 6 * D])
        gates = sb("gates_made", [128, B, 2 * D])
        cT = sb("cT", [128, KC, B])
        en = sb("en", [128, KC, B])
        silu = sb("silu", [128, KC, B])
        siluB = sb("siluB", [128, KC, B, 128])
        sgn = sb("sgn", [128, 512])
        mag = sb("mag", [128, 512])
        cI = sb("cI", [128, N], I32)
        xt = sb("xt", [128, 8, D])
        st = sb("st", [128, 8, 6])
        mv = sb("mv", [128, 8, 2])
        rs = sb("rs", [128, 8])
        xn = sb("xn", [128, 8, D])
        hT = sb("hTa", [128, KC, N])
        hi = sb("hTa_hi", [128, KC, N], F32R)
        lo = sb("hTa_lo", [128, KC, N], F32R)
        eps = sb("eps", [128, 1])
        pm = ctx.enter_context(nc.psum_tensor("pm", [128, 512], FP32))
        pg = [ctx.enter_context(nc.psum_tensor(f"pg{i}", [128, 512], FP32)) for i in range(2)]
        pt = [ctx.enter_context(nc.psum_tensor(f"pt{i}", [128, 512], FP32)) for i in range(4)]
        loaded = sem("a_loaded")
        x_loaded = sem("a_x_loaded")
        exp_done = sem("a_exp")
        silu_done = sem("a_silu")
        mod_done = sem("a_mod")
        gate_mm = sem("a_gate_mm")
        modT_ready = sem("a_modT")
        chain = sem("a_chain")
        consts_made = sem("a_consts")
        std_done = sem("a_std")
        var_done = sem("a_var")
        norm_done = sem("a_norm")
        tr_done = sem("a_tr")
        h_done = sem("a_h")
        stored = sem("a_stored")
        lo_done = sem("a_lo")
        gates_stored = sem("a_gates_stored")
        gate_used = sem("a_gate_used")
        block = ctx.enter_context(nc.Block())

        @block.sync
        def _(sp):
            with nc.allow_non_contiguous_dma("1024 floats of the condition, once"):
                for k in range(KC):
                    sp.dma_start(cT[:, k, :], c[:, k * 128:(k + 1) * 128].rearrange("b p -> p b")).then_inc(loaded, 16)
            sp.dma_start(wm[:, :, :], wmod.rearrange("(k p) n -> p k n", p=128)).then_inc(loaded, 16)
            with sp.Fori(0, B) as b:
                sp.dma_start(xt[:, :, :], x[bass.ds(b, 1)].rearrange("a (t p) d -> p (a t) d", p=128)).then_inc(x_loaded, 16)
                sp.wait_ge(h_done, 4 * b + 4)
                sp.wait_ge(lo_done, 4 * b + 4)
                apart(sp, spare)
                for part, src in enumerate((hi, lo)):
                    sp.dma_start(hT_d[bass.ds(b, 1), part].rearrange("a p k n -> p (a k) n"), src[:, :, :].bitcast(FP32)).then_inc(stored, 16)
                sp.wait_ge(stored, 32 * b + 32)
                apart(sp, spare)
            sp.wait_ge(gate_used, B)
            sp.dma_start(gates_d, gates[:, :, :]).then_inc(gates_stored, 16)
            sp.wait_ge(gates_stored, 16)

        @block.gpsimd
        def _(gp):
            gp.memset(consts["one"][:, :], 1.0).then_inc(consts_made, 1)
            gp.memset(ident[:, :], 0.0).then_inc(consts_made, 1)
            gp.wait_ge(consts_made, 2)
            gp.affine_select(out=ident[:, :], in_=ident[:, :], compare_op=ALU.not_equal, fill=1.0, base=0,
                             pattern=[[-1, 128]], channel_multiplier=1).then_inc(consts_made, 1)
            gp.iota(cI[:, :], pattern=[[-1, N]], base=N - 1, channel_multiplier=0).then_inc(consts_made, 1)
            gp.wait_ge(consts_made, 4)
            gp.tensor_scalar(cM[:, :], cI[:, :], MAGIC, None, ALU.add).then_inc(consts_made, 1)
            with gp.Fori(0, B) as b:
                for i in range(4):
                    k, cols = i // 2, slice((i % 2) * 512, (i % 2) * 512 + 512)
                    gp.wait_ge(h_done, 4 * b + i + 1)
                    gp.tensor_tensor(lo[:, k, cols], hT[:, k, cols], hi[:, k, cols].bitcast(FP32), ALU.subtract).then_inc(lo_done, 1)

        @block.scalar
        def _(act):
            act.wait_ge(loaded, 48)
            act.activation(en[:, :, :], cT[:, :, :], ACT.Exp, scale=-1.0).then_inc(exp_done, 1)
            act.wait_ge(modT_ready, 1)
            with act.Fori(0, B) as b:
                act.wait_ge(var_done, b + 1)
                ge(act, stored, 32 * b)
                act.activation(rs[:, :], mv[:, :, 1], ACT.Sqrt, bias=eps[:, 0:1]).then_inc(std_done, 1)
                for i in range(4):
                    k = i // 2
                    act.wait_ge(tr_done, 4 * b + i + 1)
                    apart(act, spare)
                    cols = slice((i % 2) * 512, (i % 2) * 512 + 512)
                    for dst in (hT, hi):
                        last = act.activation(dst[:, k, cols], pt[i][:, :], ACT.Identity,
                                              scale=modT[:, 2 + k, bass.ds(b, 1)], bias=modT[:, k, bass.ds(b, 1)])
                    last.then_inc(h_done, 1)

        @block.tensor
        def _(pe):
            pe.wait_ge(silu_done, 1)
            for ch in range(12):
                for k in range(KC):
                    last = pe.matmul(pm[:, ch * B:(ch + 1) * B], wm[:, k, ch * 128:(ch + 1) * 128], silu[:, k, :],
                                     start=(k == 0), stop=(k == KC - 1))
            last.then_inc(mod_done, 1)
            pe.wait_ge(silu_done, 2)
            for b in range(B):
                ge(pe, gate_used, b - 1)
                for i, part in enumerate((2, 5)):
                    for k in range(KC):
                        last = pe.matmul(pg[b % 2][:, i * D:(i + 1) * D], siluB[:, k, b, :],
                                         wm[:, k, part * D:(part + 1) * D], start=(k == 0), stop=(k == KC - 1))
                last.then_inc(gate_mm, 1)
            pe.wait_ge(consts_made, 3)
            with pe.Fori(0, B) as b:
                pe.wait_ge(norm_done, b + 1)
                for i in range(4):
                    k, half = i // 2, i % 2
                    for t in range(4):
                        last = pe.transpose(pt[i][:, t * 128:(t + 1) * 128],
                                            xn[:, half * 4 + t, k * 128:(k + 1) * 128], ident[:, :])
                    last.then_inc(tr_done, 1)

        @block.vector
        def _(dve):
            done = [0]

            def link(ins):
                done[0] += 1
                ins.then_inc(chain, 1)
                dve.wait_ge(chain, done[0])

            link(dve.memset(eps[:, :], EPS))
            dve.wait_ge(exp_done, 1)
            link(dve.tensor_scalar(en[:, :, :], en[:, :, :], 1.0, None, ALU.add))
            link(dve.reciprocal(en[:, :, :], en[:, :, :]))
            dve.tensor_tensor(silu[:, :, :], cT[:, :, :], en[:, :, :], ALU.mult).then_inc(silu_done, 1)
            dve.wait_ge(silu_done, 1)
            dve.tensor_copy(siluB[:, :, :, :], silu[:, :, :].unsqueeze(3).broadcast_to([128, KC, B, 128])).then_inc(silu_done, 1)
            dve.wait_ge(mod_done, 1)
            link(dve.tensor_copy(modT[:, :, :], pm[:, 0:12 * B].rearrange("p (m b) -> p m b", b=B)))
            link(dve.tensor_scalar(modT[:, 2:4, :], modT[:, 2:4, :], 1.0, None, ALU.add))
            dve.tensor_scalar(modT[:, 8:10, :], modT[:, 8:10, :], 1.0, None, ALU.add).then_inc(modT_ready, 1)
            for b in range(B):
                dve.wait_ge(gate_mm, b + 1)
                link(dve.tensor_scalar(sgn[:, :], pg[b % 2][:, :], 0.0, 2.0, ALU.is_ge, ALU.mult))
                link(dve.tensor_scalar(mag[:, :], pg[b % 2][:, :], -1.0, None, ALU.mult))
                link(dve.tensor_tensor(mag[:, :], mag[:, :], pg[b % 2][:, :], ALU.max))
                link(dve.tensor_scalar(mag[:, :], mag[:, :], 0.25, None, ALU.max))
                dve.scalar_tensor_tensor(gates[:, b, :], sgn[:, :], -1.0, mag[:, :], ALU.add, ALU.mult).then_inc(gate_used, 1)
                dve.wait_ge(gate_used, b + 1)
            base = done[0]
            dve.wait_ge(chain, base)
            per = 2
            with dve.Fori(0, B) as b:
                dve.wait_ge(x_loaded, 16 * b + 16)
                for t in range(8):
                    last = dve.bn_stats(st[:, t, :], xt[:, t, :])
                last.then_inc(chain, 1)
                dve.wait_ge(chain, base + per * b + 1)
                apart(dve, spare)
                for t in range(8):
                    last = dve.bn_aggr(mv[:, t, :], st[:, t, :])
                last.then_inc(var_done, 1)
                dve.wait_ge(std_done, b + 1)
                dve.reciprocal(rs[:, :], rs[:, :]).then_inc(chain, 1)
                dve.wait_ge(chain, base + per * b + 2)
                dve.wait_ge(var_done, b + 1)
                for t in range(8):
                    last = dve.tensor_scalar(xn[:, t, :], xt[:, t, :], mv[:, t, 0:1], rs[:, t:t + 1], ALU.subtract, ALU.mult)
                last.then_inc(norm_done, 1)
                dve.wait_ge(norm_done, b + 1)
                dve.wait_ge(tr_done, 4 * b + 4)


def attention(nc, m, blk, hT_d, Wq, Wkv, attnT_d, recip_d, consts, tag, NB, W, ZW, guard=None):
    ident, cM, minpos, spare = (consts[k] for k in ("ident", "cM", "minpos", "spare"))
    IW = NB * 128
    UH = N // IW
    UP = 2 * UH
    UB = 2 * UP
    FAR = N - W
    FCH = (N - ZW) // 128
    NEAR = CHUNKS - FCH
    EX = ZW - W
    sem = lambda n: m.sem(f"{tag}_{n}")
    S_ready, S_act, S_max = sem("S_ready"), sem("S_act"), sem("S_max")
    A_ready, A_step = sem("A_ready"), sem("A_step")
    fM_read, X_ready, rise_ready = sem("fM_read"), sem("X_ready"), sem("rise_ready")
    B_step = sem("B_step")
    far_bias, z_ready = sem("far_bias"), sem("z_ready")
    row_mm, row_set = sem("row_mm"), sem("row_set")
    T_ready, exp_done, pv_done = sem("T_ready"), sem("exp_done"), sem("pv_done")
    O_copied, sums_turned, recip_made = sem("O_copied"), sem("sums_turned"), sem("recip_made")
    recip_stored, recip_spread, out_ready = sem("recip_stored"), sem("recip_spread"), sem("out_ready")
    stored = [sem("stored_even"), sem("stored_odd")]
    loaded, w_hi, w_lo = sem("loaded"), sem("w_hi"), sem("w_lo")
    proj_mm, proj_set, lo_set, D_ready = sem("proj_mm"), sem("proj_set"), sem("lo_set"), sem("D_ready")
    whole_set = sem("whole_set")
    z_shifted, nf_hi, logits_summed = sem("z_shifted"), sem("nf_hi"), sem("logits_summed")
    s16_ready, w_ready, cross_zeroed = sem("s16_ready"), sem("w_ready"), sem("cross_zeroed")
    USES = [("q", 0, 0), ("q", 0, 1), ("k", 0, 0), ("k", 0, 1),
            ("q", 1, 0), ("q", 1, 1), ("k", 1, 0), ("k", 1, 1), ("E", 0, 0), ("v", 0, 0), ("v", 0, 1), ("E", 1, 0)]
    PJ = len(USES)
    SHARE = {1: range(0, 4), 2: range(4, 9), 3: range(9, 12)}
    LEFT = SHARE[3] if UP == 4 else ()

    def v3(t):
        return t[:, 0:NB * W].rearrange("p (t w) -> p t w", w=W)

    Tb, fM = v3(m.Tb), v3(m.fM)
    Ps = [v3(t) for t in m.P]
    w_, s16, cross, X = ([v3(t) for t in ts] for ts in (m.w, m.s16, m.cross, m.X))
    mk = [v3(t) for t in m.mk]
    zs = [t[:, 0:NB * ZW].rearrange("p (t w) -> p t w", w=ZW) for t in m.zs]
    fmax, zmax, nfar, negm, mcol = m.fmax, m.zmax, m.nfar, m.negm, m.mcol

    def place(s):
        return s // UP % 2, s % UP // UH, s % UH

    KA = 4
    KM = 12
    KB = KM + 3 + (4 if FAR else 0)
    nbody = PAIRS // 2
    FIRST, LATER = list(range(NB))[:2], [list(range(NB))[2:3], list(range(NB))[3:4]]

    def load_pair(sp, n):
        ge(sp, proj_mm, PJ * n)
        apart(sp, spare)
        bi, p = n // (H // 2), n % (H // 2)
        for part in range(2):
            sp.dma_start(m.hTb[part][:, :, :].bitcast(FP32), hT_d[bass.ds(bi, 1), part].rearrange("a p k n -> p (a k) n")).then_inc(loaded, 16)
        for i, (src, off) in enumerate(((Wq, 0), (Wkv, 0), (Wkv, H * DH))):
            sp.dma_start(m.wp[:, :, i, :],
                         src.rearrange("(k p) n -> p k n", p=128)[:, :, bass.ds(p * 128 + off, 128)]).then_inc(loaded, 16)

    LD = 5 * 16

    def split_index(i):
        return sum(what in "qk" for what, _, _ in USES[:i])

    def twice_in(k):
        heads = m.wp[:, k, 0:2, :].rearrange("p w (h d) -> p (w h) d", h=2)
        return heads.unsqueeze(2).broadcast_to([128, 4, 2, DH])

    def twice_out(ws, k):
        return ws[:, k, 0:4, :].rearrange("p j (r d) -> p j r d", r=2)

    def bank_free(pe, rows, uses):
        ge(pe, row_set, rows)
        ge(pe, proj_set, uses)

    def pe_project(pe, n, pp, i, rows):
        (hh, hl), (wh, wl) = m.hTb, m.ws
        bank_free(pe, rows, PJ * n + i)
        if i == 0:
            pe.wait_ge(loaded, LD * n + LD)
            pe.wait_ge(w_hi, n + 1)
            pe.wait_ge(w_lo, n + 1)
        what, h, half = USES[i]
        if what in "qk":
            for j, (w, x, k) in enumerate((w, x, k) for k in range(KC) for w in (wh, wl) for x in (hh, hl)):
                last = pe.matmul(m.pM[:, :], w[:, k, 2 * (what == "k") + h, :], x[:, k, half * 512:half * 512 + 512],
                                 start=(j == 0), stop=(j == 4 * KC - 1))
        elif what == "v":
            for t in range(4):
                tok = (half * 4 + t) * 128
                for j, (w, x, k) in enumerate((w, x, k) for k in range(KC) for x in (hh, hl) for w in (wh, wl)):
                    last = pe.matmul(m.pM[:, t * 128:(t + 1) * 128], x[:, k, tok:tok + 128], w[:, k, 4, :],
                                     start=(j == 0), stop=(j == 4 * KC - 1))
        else:
            pe.wait_ge(lo_set, 8 * n + 4 * h + 2)
            for t in range(8):
                for j, pos in enumerate(m.pos):
                    last = pe.matmul(m.pM[:, t * PTS:(t + 1) * PTS], m.qs[pp][h][:, t * 128:(t + 1) * 128],
                                     pos[:, :], start=(j == 0), stop=(j == 1))
        last.then_inc(proj_mm, 1)

    def pe_scores(pe, g, s, n, tiles):
        pp, h, part = place(s)
        if s % UP == 0 and 0 in tiles:
            pe.wait_ge(lo_set, 8 * n + 8)
        for t in tiles:
            i = g * NB + t
            ge(pe, S_act, i - 1)
            if FAR:
                ge(pe, S_max, i - 1)
            for half in range(2):
                for j, ks in enumerate(m.ks[pp][h]):
                    last = pe.matmul(m.pS[(s * NB + t) % 2][:, half * 512:half * 512 + 512],
                                     m.qs[pp][h][:, part * IW + t * 128:part * IW + (t + 1) * 128],
                                     ks[:, half * 512:half * 512 + 512], start=(j == 0), stop=(j == 1))
            last.then_inc(S_ready, 1)

    def pe_values(pe, g, s, uses, between, later):
        pp, h, part = place(s)
        if FCH:
            pe.wait_ge(far_bias, g + 1)
            bank_free(pe, g, uses)
            for t in range(NB):
                last = pe.matmul(m.pM[:, t * 128:(t + 1) * 128], m.nf[s % 2][:, t, :], m.identR[:, :], start=True, stop=True)
            last.then_inc(row_mm, 1)
            later(0)
            pe.wait_ge(row_set, g + 1)

        def logits(c):
            n = g * CHUNKS + c
            ge(pe, exp_done, n - 1)
            bank = m.pT[c % 2]
            if c < FCH:
                for j, ks in enumerate(m.ks[pp][h]):
                    pe.matmul(bank[:, 0:IW], ks[:, c * 128:(c + 1) * 128], m.qs[pp][h][:, part * IW:(part + 1) * IW],
                              start=(j == 0), stop=False)
                last = pe.matmul(bank[:, 0:IW], m.onesR[:, :], m.rb[:, 0:IW], start=False, stop=True)
            else:
                if c == FCH:
                    pe.wait_ge(z_shifted, g + 1)
                for t in range(NB):
                    last = pe.transpose(bank[:, t * 128:(t + 1) * 128],
                                        zs[s % 4][:, t, (c - FCH) * 128:(c - FCH + 1) * 128], ident[:, :])
            last.then_inc(T_ready, 1)

        logits(0)
        logits(1)
        later(1)
        ge(pe, O_copied, g)
        for c in range(CHUNKS):
            pe.wait_ge(exp_done, g * CHUNKS + c + 1)
            pe.matmul(m.pO[0:DH + 1, 0:IW], m.va[pp][:, c, h, :], m.pr[c % RING][:, 0:IW], start=(c == 0),
                      stop=(c == CHUNKS - 1)).then_inc(pv_done, 1)
            if c + 2 < CHUNKS:
                logits(c + 2)
            between(c)

    def act_scores(act, g, s, tiles):
        if 0 in tiles:
            ge(act, A_ready, g)
            ge(act, T_ready, (g - 3) * CHUNKS)
        for t in tiles:
            act.wait_ge(S_ready, g * NB + t + 1)
            sl = m.pS[(s * NB + t) % 2]
            act.activation(Tb[:, t, :], sl[:, FAR:N], ACT.Tanh, scale=0.5)
            act.activation(zs[s % 4][:, t, :], sl[:, N - ZW:N], ACT.Copy).then_inc(S_act, 1)

    def act_whole(act, g, s):
        par = s % 2
        act.wait_ge(A_ready, g + 1)
        ge(act, z_ready, g - 1)
        act.activation(w_[par], fM, ACT.Identity, bias=m.minus_magic[:, 0:1]).then_inc(whole_set, 1)

    def act_weights(act, n):
        act.wait_ge(loaded, LD * n + LD)
        ge(act, proj_mm, PJ * n)
        for k in range(KC):
            act.activation(twice_out(m.ws[0], k), twice_in(k), ACT.Copy)
        act.activation(m.ws[0][:, :, 4, :], m.wp[:, :, 2, :], ACT.Copy).then_inc(w_hi, 1)

    def act_project(act, n, pp, i):
        act.wait_ge(proj_mm, PJ * n + i + 1)
        what, h, half = USES[i]
        if what in "qk":
            cols, turn = slice(half * 512, half * 512 + 512), split_index(i)
            scale = DH ** -0.5 if what == "q" else 1.0
            ge(act, lo_set, 8 * n + turn - 3)
            act.activation(m.raw[turn % 4][:, :], m.pM[:, :], ACT.Copy, scale=scale)
            dst = m.qs[pp][h] if what == "q" else m.ks[pp][h][0]
            last = act.activation(dst[:, cols], m.pM[:, :], ACT.Copy, scale=scale)
        elif what == "v":
            t = half * 4
            last = act.activation(m.va[pp][:, t:t + 4, :, 0:DH],
                                  m.pM[:, :].rearrange("p (t h d) -> p t h d", t=4, h=2), ACT.Copy)
        else:
            last = act.activation(m.ER[pp][h][:, :, :], m.pM[:, :].rearrange("p (t d) -> p t d", t=8), ACT.Copy)
        last.then_inc(proj_set, 1)

    def act_values(act, g, s, between, later, whole):
        if FCH:
            act.wait_ge(row_mm, g + 1)
            act.activation(m.rb[:, 0:IW], m.pM[0:DH, 0:IW], ACT.Copy).then_inc(row_set, 1)
            later(0)

        def shift():
            act.wait_ge(z_ready, g + 1)
            for t in range(NB):
                z = zs[s % 4]
                if EX:
                    act.activation(z[:, t, 0:EX], z[:, t, 0:EX], ACT.Identity, bias=nfar[s % 2][:, t:t + 1])
                last = act.activation(z[:, t, EX:ZW], z[:, t, EX:ZW], ACT.Identity, bias=negm[s % 2][:, t:t + 1])
            last.then_inc(z_shifted, 1)

        shift_before = max(FCH - 3, 0)
        for c in range(CHUNKS):
            if c == shift_before:
                shift()
            n = g * CHUNKS + c
            act.wait_ge(T_ready, n + 1)
            ge(act, pv_done, n + 1 - RING)
            act.activation(m.pr[c % RING][:, 0:IW], m.pT[c % 2][:, 0:IW], ACT.Exp).then_inc(exp_done, 1)
            if c == 0:
                later(1)
            if c:
                between(c - 1)
            if c == 4:
                whole()
        act.wait_ge(pv_done, (g + 1) * CHUNKS)
        ge(act, out_ready, g - 1)
        act.activation(m.oraw[s % 2][:, 0:IW], m.pO[0:DH + 1, 0:IW], ACT.Copy).then_inc(O_copied, 1)

    def pool_table(gp, n, pp, i):
        h = USES[i][1]
        gp.wait_ge(proj_set, PJ * n + i + 1)
        gp.tensor_tensor(m.DR[pp][h][:, :, 1:PTS], m.ER[pp][h][:, :, 0:PTS - 1], m.ER[pp][h][:, :, 1:PTS],
                         ALU.subtract).then_inc(D_ready, 1)
        gp.wait_ge(D_ready, 2 * n + h + 1)

    def pool_weights(gp, n):
        gp.wait_ge(w_hi, n + 1)
        for k in range(KC):
            gp.tensor_tensor(twice_out(m.ws[1], k), twice_in(k), twice_out(m.ws[0], k).bitcast(FP32), ALU.subtract)
        gp.tensor_tensor(m.ws[1][:, :, 4, :], m.wp[:, :, 2, :], m.ws[0][:, :, 4, :].bitcast(FP32), ALU.subtract).then_inc(w_lo, 1)

    def pool_low(gp, n, pp, i):
        what, h, half = USES[i]
        cols, turn = slice(half * 512, half * 512 + 512), split_index(i)
        gp.wait_ge(proj_set, PJ * n + i + 1)
        raw = m.raw[turn % 4]
        if what == "q":
            q = m.qs[pp][h][DH:128, cols]
            gp.tensor_tensor(q, raw[DH:128, :], q.bitcast(FP32), ALU.subtract).then_inc(lo_set, 1)
        else:
            gp.tensor_tensor(m.ks[pp][h][1][:, cols], raw[:, :], m.ks[pp][h][0][:, cols].bitcast(FP32),
                             ALU.subtract).then_inc(lo_set, 1)
        gp.wait_ge(lo_set, 8 * n + turn + 1)

    def pool_project(gp, n, pp, g, uses):
        gp.wait_ge(w_lo, n + 1)
        ge(gp, w_ready, g)
        ge(gp, rise_ready, g - 1)
        ge(gp, out_ready, g - 3)
        for i in uses:
            if USES[i][0] == "E":
                pool_table(gp, n, pp, i)
            elif USES[i][0] in "qk":
                pool_low(gp, n, pp, i)

    def pool_out(gp, g, s):
        gp.wait_ge(recip_spread, 16 * (g + 1))
        ge(gp, stored[s % 2], 16 * (g // 2))
        gp.tensor_tensor(m.oT[s % 2][:, 0:IW], m.oraw[s % 2][0:DH, 0:IW], m.rc[:, 0:IW], ALU.mult).then_inc(out_ready, 1)

    def pool_unit(gp, g, s, n):
        pp, h, part = place(s)
        par = s % 2
        gp.wait_ge(A_ready, g + 1)
        ge(gp, z_ready, g - 1)
        gp.tensor_tensor(cross[par][:, :, 0:W - 1], fM[:, :, 0:W - 1], fM[:, :, 1:W], ALU.subtract).then_inc(fM_read, 1)
        gp.wait_ge(D_ready, 2 * n + h + 1)
        apart(gp, spare)
        for t in range(NB):
            last = gp.tensor_copy(X[par][:, t, :].rearrange("p (r u) -> p r u", u=PTS),
                                  m.DR[pp][h][:, part * NB + t, :].unsqueeze(1).broadcast_to([128, W // PTS, PTS]))
        last.then_inc(X_ready, 1)

    def pool_fraction(gp, g, s):
        gp.wait_ge(whole_set, g + 1)
        gp.tensor_tensor(w_[s % 2], w_[s % 2], Ps[s % 2], ALU.subtract).then_inc(w_ready, 1)

    def pool_rise(gp, g, s):
        par = s % 2
        gp.wait_ge(w_ready, g + 1)
        gp.wait_ge(B_step, KB * g + KM)
        gp.tensor_tensor(w_[par], w_[par], X[par], ALU.mult).then_inc(rise_ready, 1)

    def dve_positions(dve, g, s):
        par = s % 2
        P = Ps[par]

        def scan(t):
            return dve.tensor_tensor_scan(Tb[:, t, ::-1], Tb[:, t, ::-1], m.one[:, 0:1].broadcast_to([128, W]), 0.0,
                                          ALU.add, ALU.add)

        for t in range(NB):
            dve.wait_ge(S_ready, g * NB + t + 1)
            sl = m.pS[(s * NB + t) % 2]
            if FAR:
                dve.reduce_max(fmax[par][:, t:t + 1], sl[:, 0:512], AX)
            dve.wait_ge(S_act, g * NB + t + 1)
            if FAR:
                dve.reduce_max(fmax[par][:, NB + t:NB + t + 1], sl[:, 512:FAR], AX).then_inc(S_max, 1)
            if t:
                scan(t - 1)
        scan(NB - 1).then_inc(A_step, 1)
        dve.wait_ge(A_step, KA * g + 1)
        dve.tensor_scalar(P, Tb, 0.5, CAP, ALU.mult, ALU.min).then_inc(A_step, 1)
        dve.wait_ge(A_step, KA * g + 2)
        dve.tensor_scalar(Tb, P, 0.5, MAGIC, ALU.subtract, ALU.add).then_inc(A_step, 1)
        dve.tensor_tensor(minpos[:, 0:NB], minpos[:, 0:NB], P[:, :, 0], ALU.min).then_inc(A_step, 1)
        ge(dve, fM_read, g)
        ge(dve, whole_set, g)
        ge(dve, s16_ready, g)
        dve.wait_ge(A_step, KA * g + 4)
        for t in range(NB):
            last = dve.tensor_tensor_scan(fM[:, t, ::-1], m.one[:, 0:1].broadcast_to([128, W]), Tb[:, t, ::-1],
                                          MAGIC - 1.0, ALU.add, ALU.min)
        last.then_inc(A_ready, 1)
        dve.wait_ge(A_ready, g + 1)
        dve.tensor_tensor(s16[par], cM[:, N - W:N].unsqueeze(1).broadcast_to([128, NB, W]), fM, ALU.subtract).then_inc(s16_ready, 1)

    def dve_logits(dve, g, s):
        pp, h, part = place(s)
        par = s % 2
        x = X[par]
        step = [0]

        def count(ins):
            step[0] += 1
            return ins.then_inc(B_step, 1)

        def after(n):
            dve.wait_ge(B_step, KB * g + n)
            apart(dve, spare)

        def link(ins):
            count(ins)
            dve.wait_ge(B_step, KB * g + step[0])

        def mask(bit):
            count(dve.tensor_scalar(mk[bit % 3], s16[par], 1 << bit, None, ALU.bitwise_and))

        dve.wait_ge(s16_ready, g + 1)
        mask(5)
        mask(4)
        dve.wait_ge(X_ready, g + 1)
        done = step[0]
        for bit in (5, 4, 3, 2, 1, 0):
            sh = 1 << bit
            after(1 if bit == 5 else 3 + 2 * (4 - bit))
            count(dve.copy_predicated(x[:, :, 0:W - sh], mk[bit % 3][:, :, 0:W - sh], x[:, :, sh:W]))
            if bit >= 2:
                mask(bit - 2)
        assert step[0] == KM
        dve.wait_ge(B_step, KB * g + KM)
        cr, P = cross[par], Ps[par]
        ge(dve, cross_zeroed, 2)
        dve.wait_ge(w_ready, g + 1)
        link(dve.tensor_tensor(cr[:, :, 0:W - 1], cr[:, :, 0:W - 1], x[:, :, 1:W], ALU.mult))
        for t in range(NB):
            last = dve.tensor_tensor_scan(P[:, t, ::-1], m.one[:, 0:1].broadcast_to([128, W]), cr[:, t, ::-1],
                                          m.ER[pp][h][:, part * NB + t, PTS - 1:PTS], ALU.mult, ALU.add)
        link(last)
        dve.wait_ge(rise_ready, g + 1)
        link(dve.tensor_tensor(P, P, w_[par], ALU.subtract))
        z = zs[s % 4]
        dve.wait_ge(S_act, (g + 1) * NB)
        apart(dve, spare)
        for t in range(NB):
            last = dve.tensor_tensor_reduce(z[:, t, EX:ZW], z[:, t, EX:ZW], P[:, t, :], 1.0, LOWEST, ALU.add, ALU.max,
                                            zmax[:, t:t + 1])
        last.then_inc(logits_summed, 1)
        dve.wait_ge(logits_summed, g + 1)
        if FAR:
            last_entry = m.ER[pp][h][:, part * NB:(part + 1) * NB, 0]
            link(dve.tensor_tensor(mcol[:, 0:NB], fmax[par][:, 0:NB], fmax[par][:, NB:2 * NB], ALU.max))
            link(dve.tensor_tensor(mcol[:, 0:NB], mcol[:, 0:NB], last_entry, ALU.add))
            link(dve.tensor_tensor(mcol[:, 0:NB], mcol[:, 0:NB], zmax[:, 0:NB], ALU.max))
            ge(dve, row_mm, g - 1)
            ge(dve, z_shifted, g - 1)
            link(dve.tensor_tensor(nfar[par][:, 0:NB], last_entry, mcol[:, 0:NB], ALU.subtract))
            dve.tensor_copy(m.nf[par][:, 0:NB, 0], nfar[par][:, 0:NB]).then_inc(nf_hi, 1)
            dve.wait_ge(nf_hi, g + 1)
            dve.tensor_tensor(m.nf[par][:, 0:NB, 32], nfar[par][:, 0:NB], m.nf[par][:, 0:NB, 0].bitcast(FP32),
                              ALU.subtract).then_inc(far_bias, 1)
            top = mcol
        else:
            top = zmax
            ge(dve, z_shifted, g - 1)
        dve.tensor_scalar(negm[par][:, 0:NB], top[:, 0:NB], -1.0, None, ALU.mult).then_inc(z_ready, 1)
        dve.wait_ge(z_ready, g + 1)
        assert step[0] == KB, (step[0], KB)

    def dve_recip(dve, g, s):
        dve.wait_ge(sums_turned, 16 * (g + 1))
        dve.reciprocal(m.rcol[:, 0:NB], m.rcol[:, 0:NB]).then_inc(recip_made, 1)
        dve.wait_ge(recip_made, g + 1)

    def body(eng_slot, it):
        for s in range(UB):
            eng_slot(it, s, it * UB + s)

    def run(eng, slot):
        body(slot, 0)
        with eng.Fori(1, nbody - 1) as it:
            body(slot, it)
        body(slot, nbody - 1)

    def older(it, s, g, back):
        if isinstance(it, int) and it * UB + s < back:
            return None
        return g - back, (s - back) % UB

    def project_at(it, s):
        half, off = s // UP, s % UP
        if off not in SHARE or (isinstance(it, int) and it == nbody - 1 and half == 1):
            return None
        return 2 * it + half + 1, (half + 1) % 2, SHARE[off]

    def weights_at(it, s):
        half, off = s // UP, s % UP
        if off != 0 or (isinstance(it, int) and it == nbody - 1 and half == 1):
            return None
        return 2 * it + half + 1

    def in_between(eng, pj, step):
        def between(c):
            if pj and c < len(pj[2]):
                step(eng, pj[0], pj[1], pj[2][c])
        return between

    def pe_all(pe):
        for i in range(PJ):
            pe_project(pe, 0, 0, i, 0)

        def slot(it, s, g):
            n = 2 * it + s // UP
            pe_scores(pe, g, s, n, FIRST)
            done_uses = PJ * (2 * it + s // UP + 1) + sum(len(uses) for off, uses in SHARE.items() if off < s % UP)
            if isinstance(it, int) and it == nbody - 1 and s // UP == 1:
                done_uses = PJ * PAIRS
            old = older(it, s, g, 2)
            pj = project_at(it, s)
            between = in_between(pe, pj, lambda e, n, pp, i: pe_project(e, n, pp, i, (g - 1) if FCH else 0))
            if old:
                pe_values(pe, *old, done_uses, between, lambda i: pe_scores(pe, g, s, n, LATER[i]))
            else:
                pe_scores(pe, g, s, n, LATER[0] + LATER[1])
                for c in range(CHUNKS):
                    between(c)
        run(pe, slot)
        for back in (2, 1):
            g = nbody * UB - back
            pe_values(pe, g, g % UB, PJ * PAIRS, lambda c: None, lambda i: None)

    def act_all(act):
        act_weights(act, 0)
        for i in range(PJ):
            act_project(act, 0, 0, i)

        def slot(it, s, g):
            act_scores(act, g, s, FIRST)
            old = older(it, s, g, 2)
            if old:
                act_values(act, *old, in_between(act, project_at(it, s), act_project),
                           lambda i: act_scores(act, g, s, LATER[i]), lambda: act_whole(act, g, s))
            else:
                act_scores(act, g, s, LATER[0] + LATER[1])
                act_whole(act, g, s)
                for i in (project_at(it, s) or (0, 0, ()))[2]:
                    act_project(act, *project_at(it, s)[:2], i)
            w = weights_at(it, s)
            if w is not None:
                act_weights(act, w)
        run(act, slot)
        for back in (2, 1):
            g = nbody * UB - back
            act_values(act, g, g % UB, lambda c: None, lambda i: None, lambda: None)

    def pool_all(gp):
        for par in range(2):
            gp.memset(cross[par][:, :, W - 1:W], 0.0).then_inc(cross_zeroed, 1)
        pool_weights(gp, 0)
        pool_project(gp, 0, 0, 0, range(PJ))

        def slot(it, s, g):
            pj = project_at(it, s - 1) if s else None
            if pj:
                pool_project(gp, pj[0], pj[1], g, pj[2])
            if s == 0 and not (isinstance(it, int) and it == 0):
                pool_project(gp, 2 * it, 0, g, LEFT)
            pool_unit(gp, g, s, 2 * it + s // UP)
            old = older(it, s, g, 1)
            if old:
                pool_rise(gp, *old)
            pool_fraction(gp, g, s)
            old = older(it, s, g, 3)
            if old:
                pool_out(gp, *old)
            w = weights_at(it, s)
            if w is not None:
                pool_weights(gp, w)
        run(gp, slot)
        pool_rise(gp, nbody * UB - 1, UB - 1)
        for back in (3, 2, 1):
            g = nbody * UB - back
            pool_out(gp, g, g % UB)

    def dve_all(dve):
        def slot(it, s, g):
            dve_positions(dve, g, s)
            old = older(it, s, g, 3)
            if old:
                dve_recip(dve, *old)
            old = older(it, s, g, 1)
            if old:
                dve_logits(dve, *old)
        run(dve, slot)
        G = nbody * UB
        dve_recip(dve, G - 3, (G - 3) % UB)
        dve_logits(dve, G - 1, (G - 1) % UB)
        dve_recip(dve, G - 2, (G - 2) % UB)
        dve_recip(dve, G - 1, (G - 1) % UB)

    def sp_sums(sp, g, s):
        sp.wait_ge(O_copied, g + 1)
        sp.dma_start(m.rcol[:, 0:NB], m.oraw[s % 2][DH:DH + 1, 0:IW]).then_inc(sums_turned, 16)

    def sp_spread(sp, g, s):
        sp.wait_ge(recip_made, g + 1)
        sp.dma_start(recip_d[s % 2, 0:IW].rearrange("(p t) -> p t", t=NB), m.rcol[:, 0:NB]).then_inc(recip_stored, 16)
        sp.wait_ge(recip_stored, 16 * (g + 1))
        sp.dma_start(m.rc[:, 0:IW], recip_d[s % 2:s % 2 + 1, 0:IW].broadcast_to([DH, IW])).then_inc(recip_spread, 16)

    def sp_store(sp, n, g, s):
        pp, h, part = place(s)
        sp.wait_ge(out_ready, g + 1)
        apart(sp, spare)
        sp.dma_start(attnT_d[bass.ds(n, 1), h, :, part * IW:(part + 1) * IW].rearrange("a d n -> (a d) n"),
                     m.oT[s % 2][:, 0:IW]).then_inc(stored[s % 2], 16)

    def sp_all(sp):
        load_pair(sp, 0)

        def slot(it, s, g):
            if s % UP == 0 and not (isinstance(it, int) and it == nbody - 1 and s // UP == 1):
                load_pair(sp, 2 * it + s // UP + 1)
            old = older(it, s, g, 3)
            if old:
                sp_sums(sp, *old)
                sp_spread(sp, *old)
                go, so = old
                sp_store(sp, 2 * it + (s - 3) // UP, go, so)
        run(sp, slot)
        for back in (3, 2, 1):
            g = nbody * UB - back
            sp_sums(sp, g, g % UB)
            sp_spread(sp, g, g % UB)
            sp_store(sp, g // UP, g, g % UB)
        for par in range(2):
            sp.wait_ge(stored[par], 16 * nbody * UB // 2)

    def guarded(eng, work):
        if guard is None:
            work(eng)
        else:
            need = eng.value_load(guard[0:1, 0:1], min_val=0, max_val=128)
            with eng.If(need != 0):
                work(eng)

    @blk.sync
    def _(sp):
        guarded(sp, sp_all)

    @blk.tensor
    def _(pe):
        guarded(pe, pe_all)

    @blk.scalar
    def _(act):
        guarded(act, act_all)

    @blk.gpsimd
    def _(gp):
        guarded(gp, pool_all)

    @blk.vector
    def _(dve):
        guarded(dve, dve_all)


def coverage(nc, m, consts, flag):
    with ExitStack() as ctx:
        minpos, low, low1, ps = consts["minpos"], m.zmax, m.mcol[:, 0:1], m.pM
        compared = ctx.enter_context(nc.semaphore("f_compared"))
        counted = ctx.enter_context(nc.semaphore("f_counted"))
        flagged = ctx.enter_context(nc.semaphore("f_flagged"))
        block = ctx.enter_context(nc.Block())

        @block.vector
        def _(dve):
            dve.tensor_scalar(low[:, :], minpos[:, :], CAP, None, ALU.is_lt).then_inc(compared, 1)
            dve.wait_ge(compared, 1)
            dve.reduce_max(low1, low[:, :], AX).then_inc(compared, 1)
            dve.wait_ge(counted, 1)
            dve.tensor_copy(flag[0:1, 0:1], ps[0:1, 0:1]).then_inc(flagged, 1)
            dve.wait_ge(flagged, 1)

        @block.tensor
        def _(pe):
            pe.wait_ge(compared, 2)
            pe.matmul(ps[0:1, 0:1], low1, consts["one"][:, :], start=True, stop=True).then_inc(counted, 1)


def feed_forward(nc, x, attnT_d, gates_d, weights, consts, out):
    Wout, b_out, gate_w, gate_b, expert_w, expert_b = weights
    ident, modT, spare = (consts[k] for k in ("ident", "modT", "spare"))
    NT = TOK // 128
    with ExitStack() as ctx:
        sb = lambda n, s, d=FP32: ctx.enter_context(nc.sbuf_tensor(n, s, d))
        sem = lambda n: ctx.enter_context(nc.semaphore(n))
        pb = lambda n: ctx.enter_context(nc.psum_tensor(n, [128, 512], FP32))
        wo = sb("wo", [128, H * DH // 128, D])
        gates = sb("gates", [128, B, 2 * D])
        ew = sb("ew", [128, KC, NE, D])
        gw = sb("gw", [128, KC, NE])
        bo = sb("bo", [128, D])
        gb = sb("gb", [128, NE])
        eb = sb("eb", [NE, D])
        aT = [sb(f"aT{i}", [128, H * DH // 128, 128]) for i in range(2)]
        xt = [sb(f"xr{i}", [128, D]) for i in range(2)]
        x1 = [sb(f"x1_{i}", [128, D]) for i in range(2)]
        y = sb("y", [128, D])
        st = sb("st2", [128, 6])
        mv = sb("mv2", [128, 2])
        sd = sb("sd", [128, 1])
        rstd = sb("rstd", [128, 1])
        xn = sb("xn2", [128, D])
        eps = sb("eps2", [128, 1])
        h2T = [sb(f"h2T{i}", [128, KC, 128]) for i in range(2)]
        lg = sb("lg", [128, NE])
        mx = sb("mx", [128, 1])
        ex = sb("ex", [128, NE])
        sm = sb("sm", [128, 1])
        rsm = sb("rsm", [128, 1])
        pr = sb("prg", [128, NE])
        sel = sb("sel", [128, NE])
        ws = sb("ws", [128, 1])
        z0 = sb("z0", [128, 1])
        rws = sb("rws", [128, 1])
        wgt = sb("wgt", [128, NE])
        wT = sb("wT", [NE, 128])
        acc = sb("acc", [128, D])
        res = [sb(f"res{i}", [128, D]) for i in range(2)]
        pY, pH, pG, pB = pb("pY"), pb("pH"), pb("pG"), pb("pB")
        pE = [pb(f"pE{i}") for i in range(4)]
        w_loaded = sem("p_w_loaded")
        in_loaded = [sem("p_in_even"), sem("p_in_odd")]
        y_mm, y_used, x1_made = sem("p_y_mm"), sem("p_y_used"), sem("p_x1")
        chain = sem("p_chain")
        var_done, std_done, norm_done = sem("p_var"), sem("p_std"), sem("p_norm")
        tr_mm, h_set = sem("p_tr"), sem("p_h")
        gate_mm, ex_in, ex_out = sem("p_gate"), sem("p_ex_in"), sem("p_ex_out")
        exp_mm, exp_used = sem("p_experts"), sem("p_experts_used")
        w_made, wT_mm, wT_set, bias_mm, acc_done = sem("p_w"), sem("p_wT"), sem("p_wTs"), sem("p_bias"), sem("p_acc")
        stored = [sem("p_stored_even"), sem("p_stored_odd")]
        eps_set = sem("p_eps")
        block = ctx.enter_context(nc.Block())
        K1, K2 = 3, 15

        def run(eng, slot):
            for s in range(2):
                slot(0, s, s)
            with eng.Fori(1, NT // 2) as it:
                for s in range(2):
                    slot(it, s, 2 * it + s)

        def tile_before(it, s):
            return not (isinstance(it, int) and it == 0 and s == 0)

        def batch_gate(i, part):
            return gates[:, bass.ds(i // (N // 128), 1), part * D:(part + 1) * D].rearrange("p a d -> p (a d)")

        @block.sync
        def _(sp):
            sp.dma_start(wo[:, :, :], Wout.rearrange("(k p) n -> p k n", p=128)).then_inc(w_loaded, 16)
            for e in range(NE):
                sp.dma_start(ew[:, :, e, :], expert_w[e].rearrange("(k p) n -> p k n", p=128)).then_inc(w_loaded, 16)
            with nc.allow_non_contiguous_dma("small weights, once"):
                sp.dma_start(gw[:, :, :], gate_w.rearrange("(k p) n -> p k n", p=128)).then_inc(w_loaded, 16)
                sp.dma_start(bo[:, :], b_out.rearrange("(a n) -> a n", a=1).broadcast_to([128, D])).then_inc(w_loaded, 16)
                sp.dma_start(gb[:, :], gate_b.rearrange("(a n) -> a n", a=1).broadcast_to([128, NE])).then_inc(w_loaded, 16)
                sp.dma_start(eb[:, :], expert_b).then_inc(w_loaded, 16)
                sp.dma_start(gates[:, :, :], gates_d).then_inc(w_loaded, 16)

            def load(i, par):
                bi, t = i // (N // 128), i % (N // 128)
                ge(sp, x1_made, i - 1)
                apart(sp, spare)
                sp.dma_start(xt[par][:, :], x.rearrange("b n d -> (b n) d")[bass.ds(i * 128, 128), :]).then_inc(in_loaded[par], 16)
                sp.dma_start(aT[par][:, :, :],
                             attnT_d.rearrange("(b k) h d n -> b (h d) k n", b=B)[
                                 bass.ds(bi, 1), :, :, bass.ds(t * 128, 128)].rearrange("a p k n -> p (a k) n")
                             ).then_inc(in_loaded[par], 16)

            def store(i, par):
                sp.wait_ge(acc_done, i + 1)
                apart(sp, spare)
                sp.dma_start(out.rearrange("b n d -> (b n) d")[bass.ds(i * 128, 128), :], res[par][:, :]).then_inc(stored[par], 16)

            def slot(it, s, i):
                load(i, s)
                if tile_before(it, s):
                    store(i - 1, 1 - s)
            run(sp, slot)
            store(NT - 1, 1)
            for par in range(2):
                sp.wait_ge(stored[par], 16 * NT // 2)

        @block.tensor
        def _(pe):
            pe.wait_ge(w_loaded, 16 * (NE + 6))

            def stage1(it, s, i):
                pe.wait_ge(in_loaded[s], 32 * (it + 1))
                ge(pe, y_used, i)
                for k in range(H * DH // 128):
                    last = pe.matmul(pY[:, 0:D], aT[s][:, k, :], wo[:, k, :], start=(k == 0), stop=(k == H * DH // 128 - 1))
                last.then_inc(y_mm, 1)

            def experts(i, s):
                h = h2T[s]
                pe.wait_ge(h_set, i + 1)
                ge(pe, wT_set, i)
                for k in range(KC):
                    last = pe.matmul(pG[:, 0:NE], h[:, k, :], gw[:, k, :], start=(k == 0), stop=(k == KC - 1))
                last.then_inc(gate_mm, 1)
                for q in range(4):
                    ge(pe, exp_used, 4 * (i - 1) + q + 1 if isinstance(i, int) else 4 * i + (q - 3))
                    for k in range(KC):
                        last = pe.matmul(pE[q][:, :], h[:, k, :], ew[:, k, 2 * q:2 * q + 2, :].rearrange("p e n -> p (e n)"),
                                         start=(k == 0), stop=(k == KC - 1))
                    last.then_inc(exp_mm, 1)

            def transposes(i):
                pe.wait_ge(norm_done, i + 1)
                ge(pe, h_set, i)
                for k in range(KC):
                    last = pe.transpose(pH[:, k * 128:(k + 1) * 128], xn[:, k * 128:(k + 1) * 128], ident[:, :])
                last.then_inc(tr_mm, 1)

            def biases(i):
                pe.wait_ge(w_made, i + 1)
                pe.transpose(pG[0:NE, 128:256], wgt[:, :], ident[:, :]).then_inc(wT_mm, 1)
                pe.wait_ge(wT_set, i + 1)
                ge(pe, acc_done, i)
                pe.matmul(pB[:, 0:D], wT[:, :], eb[:, :], start=True, stop=True).then_inc(bias_mm, 1)

            def slot(it, s, i):
                stage1(it, s, i)
                if tile_before(it, s):
                    experts(i - 1, 1 - s)
                transposes(i)
                if tile_before(it, s):
                    biases(i - 1)
            run(pe, slot)
            experts(NT - 1, 1)
            biases(NT - 1)

        @block.scalar
        def _(act):
            def stage1(i, s):
                act.wait_ge(var_done, i + 1)
                act.activation(sd[:, :], mv[:, 1:2], ACT.Sqrt, bias=eps[:, 0:1]).then_inc(std_done, 1)

            def turned(i, s):
                act.wait_ge(tr_mm, i + 1)
                ge(act, exp_mm, 4 * (i - 1))
                apart(act, spare)
                bi = i // (N // 128)
                for k in range(KC):
                    last = act.activation(h2T[s][:, k, :], pH[:, k * 128:(k + 1) * 128], ACT.Identity,
                                          scale=modT[:, 8 + k, bass.ds(bi, 1)], bias=modT[:, 6 + k, bass.ds(bi, 1)])
                last.then_inc(h_set, 1)

            def stage2(i):
                act.wait_ge(ex_in, i + 1)
                act.activation(ex[:, :], lg[:, :], ACT.Exp, accum_out=sm[:, :]).then_inc(ex_out, 1)
                act.wait_ge(wT_mm, i + 1)
                ge(act, bias_mm, i)
                act.activation(wT[:, :], pG[0:NE, 128:256], ACT.Copy).then_inc(wT_set, 1)

            act.wait_ge(eps_set, 1)

            def slot(it, s, i):
                stage1(i, s)
                turned(i, s)
                if tile_before(it, s):
                    stage2(i - 1)
            run(act, slot)
            stage2(NT - 1)

        @block.vector
        def _(dve):
            dve.memset(eps[:, :], EPS).then_inc(eps_set, 1)
            dve.wait_ge(w_loaded, 16 * (NE + 6))

            def stage1(it, s, i):
                step = [0]

                def link(ins):
                    step[0] += 1
                    ins.then_inc(chain, 1)
                    dve.wait_ge(chain, K1 * i + K2 * (i - 1 if tile_before(it, s) else 0) + step[0])

                dve.wait_ge(in_loaded[s], 32 * (it + 1))
                dve.wait_ge(y_mm, i + 1)
                dve.tensor_tensor(y[:, :], pY[:, 0:D], bo[:, :], ALU.add).then_inc(y_used, 1)
                dve.wait_ge(y_used, i + 1)
                link(dve.tensor_tensor(y[:, :], y[:, :], batch_gate(i, 0), ALU.mult))
                dve.tensor_tensor(x1[s][:, :], y[:, :], xt[s][:, :], ALU.add).then_inc(x1_made, 1)
                dve.wait_ge(x1_made, i + 1)
                link(dve.bn_stats(st[:, :], x1[s][:, :]))
                ge(dve, std_done, i)
                apart(dve, spare)
                dve.bn_aggr(mv[:, :], st[:, :]).then_inc(var_done, 1)
                dve.wait_ge(std_done, i + 1)
                link(dve.reciprocal(rstd[:, :], sd[:, :]))
                ge(dve, tr_mm, i)
                dve.wait_ge(var_done, i + 1)
                dve.tensor_scalar(xn[:, :], x1[s][:, :], mv[:, 0:1], rstd[:, 0:1], ALU.subtract, ALU.mult).then_inc(norm_done, 1)
                dve.wait_ge(norm_done, i + 1)
                assert step[0] == K1

            def stage2(i, s):
                step = [0]

                def link(ins):
                    step[0] += 1
                    ins.then_inc(chain, 1)
                    dve.wait_ge(chain, K1 * (NT if isinstance(i, int) and i == NT - 1 else i + 2) + K2 * i + step[0])

                dve.wait_ge(gate_mm, i + 1)
                link(dve.tensor_tensor(lg[:, :], pG[:, 0:NE], gb[:, :], ALU.add))
                link(dve.reduce_max(mx[:, :], lg[:, :], AX))
                dve.tensor_scalar(lg[:, :], lg[:, :], mx[:, 0:1], None, ALU.subtract).then_inc(ex_in, 1)
                dve.wait_ge(ex_out, i + 1)
                link(dve.reciprocal(rsm[:, :], sm[:, :]))
                link(dve.tensor_scalar(pr[:, :], ex[:, :], rsm[:, 0:1], None, ALU.mult))
                link(dve.scalar_tensor_tensor(sel[:, :], pr[:, :], THRESHOLD, pr[:, :], ALU.is_ge, ALU.mult))
                link(dve.reduce_sum(ws[:, :], sel[:, :], AX))
                link(dve.tensor_scalar(z0[:, :], ws[:, :], 0.0, None, ALU.is_equal))
                link(dve.tensor_tensor(ws[:, :], ws[:, :], z0[:, :], ALU.add))
                link(dve.reciprocal(rws[:, :], ws[:, :]))
                ge(dve, wT_mm, i)
                dve.tensor_scalar(wgt[:, :], sel[:, :], rws[:, 0:1], None, ALU.mult).then_inc(w_made, 1)
                dve.wait_ge(w_made, i + 1)
                for e in range(NE):
                    if e % 2 == 0:
                        dve.wait_ge(exp_mm, 4 * i + e // 2 + 1)
                    src = pE[e // 2][:, (e % 2) * D:(e % 2 + 1) * D]
                    if e == 0:
                        link(dve.tensor_scalar(acc[:, :], src, wgt[:, 0:1], None, ALU.mult))
                    elif e % 2 == 0:
                        link(dve.scalar_tensor_tensor(acc[:, :], src, wgt[:, e:e + 1], acc[:, :], ALU.mult, ALU.add))
                    else:
                        dve.scalar_tensor_tensor(acc[:, :], src, wgt[:, e:e + 1], acc[:, :], ALU.mult, ALU.add).then_inc(exp_used, 1)
                        dve.wait_ge(exp_used, 4 * i + e // 2 + 1)
                dve.wait_ge(bias_mm, i + 1)
                link(dve.tensor_tensor(acc[:, :], acc[:, :], pB[:, 0:D], ALU.add))
                link(dve.tensor_tensor(acc[:, :], acc[:, :], batch_gate(i, 1), ALU.mult))
                ge(dve, stored[s], 16 * (i // 2))
                dve.tensor_tensor(res[s][:, :], acc[:, :], x1[s][:, :], ALU.add).then_inc(acc_done, 1)
                dve.wait_ge(acc_done, i + 1)
                assert step[0] == K2, step[0]

            def slot(it, s, i):
                stage1(it, s, i)
                if tile_before(it, s):
                    stage2(i - 1, 1 - s)
            run(dve, slot)
            stage2(NT - 1, 1)


class Buffers:

    def __init__(self, nc, ctx):
        sb = lambda n, s, d=FP32: ctx.enter_context(nc.sbuf_tensor(n, s, d))
        pb = lambda n, w=512: ctx.enter_context(nc.psum_tensor(n, [128, w], FP32))
        two = lambda n, s, d=FP32: [sb(f"{n}{i}", s, d) for i in range(2)]
        self.sem = lambda n: ctx.enter_context(nc.semaphore(n))
        self.hTb = two("hTb", [128, KC, N], F32R)
        self.wp = sb("wp", [128, KC, 3, 128])
        self.ws = two("ws", [128, KC, 5, 128], F32R)
        self.raw = [sb(f"raw{i}", [128, 512]) for i in range(4)]
        self.qs = [two(f"qs{p}", [128, N], F32R) for p in range(2)]
        self.ks = [[[sb(f"ks{p}{h}{i}", [128, N], F32R) for i in range(2)] for h in range(2)] for p in range(2)]
        self.va = two("va", [128, CHUNKS, 2, DH + 1])
        self.ER = [two(f"ER{p}", [128, CHUNKS, PTS]) for p in range(2)]
        self.DR = [two(f"DR{p}", [128, CHUNKS, PTS]) for p in range(2)]
        self.pos = two("pos_parts", [128, PTS], F32R)
        self.identR = sb("identR", [128, 128], F32R)
        self.onesR = sb("onesR", [DH, 128], F32R)
        self.nf = two("nf", [128, 4, 128], F32R)
        self.rb = sb("rb", [DH, 512], F32R)
        self.Tb, self.fM, self.P = sb("Tb", [128, N]), sb("fM", [128, N]), two("P", [128, N])
        self.w, self.cross, self.X = two("w", [128, N]), two("cross", [128, N]), two("X", [128, N])
        self.s16, self.mk = two("s16", [128, N], I16), [sb(f"mk{i}", [128, N], I16) for i in range(3)]
        self.zs = [sb(f"zs{i}", [128, N]) for i in range(4)]
        self.fmax, self.nfar, self.negm = two("fmax", [128, 8]), two("nfar", [128, 4]), two("negm", [128, 4])
        self.zmax, self.mcol = sb("zmax", [128, 8]), sb("mcol", [128, 8])
        self.pr = [sb(f"pr{i}", [128, 512]) for i in range(RING)]
        self.oraw, self.rc, self.oT = two("oraw", [DH + 1, 512]), sb("rc", [DH, 512]), two("oT", [DH, 512])
        self.rcol = sb("rcol", [128, 4])
        self.minus_magic = sb("minus_magic", [128, 1])
        self.pS, self.pT = [pb(f"pS{i}", N) for i in range(2)], [pb(f"pT{i}") for i in range(2)]
        self.pO, self.pM = pb("pO"), pb("pM")


def fill(nc, m, pos_emb, consts):
    with ExitStack() as ctx:
        pos = m.pr[0][:, 0:PTS]
        pos8 = m.pr[1][:, 0:PTS]
        loaded = ctx.enter_context(nc.semaphore("i_loaded"))
        filled = ctx.enter_context(nc.semaphore("i_filled"))
        block = ctx.enter_context(nc.Block())

        @block.sync
        def _(sp):
            for half in range(2):
                sp.dma_start(pos[half * DH:(half + 1) * DH, :], pos_emb).then_inc(loaded, 16)
            sp.wait_ge(loaded, 32)

        @block.vector
        def _(dve):
            done = [0]

            def link(ins):
                done[0] += 1
                ins.then_inc(filled, 1)
                dve.wait_ge(filled, done[0])

            link(dve.memset(consts["minpos"][:, :], CAP + 1.0))
            link(dve.memset(m.minus_magic[:, :], -MAGIC))
            dve.wait_ge(loaded, 32)
            link(dve.tensor_scalar(pos8, pos[:, ::-1], float(DH) ** 0.5, None, ALU.mult))
            link(dve.tensor_copy(m.pos[0][:, :], pos8))
            link(dve.tensor_tensor(m.pos[1][:, :], pos8, m.pos[0][:, :].bitcast(FP32), ALU.subtract))
            link(dve.tensor_copy(m.identR[:, :], consts["ident"][:, :]))
            link(dve.tensor_scalar(m.nf[0][:, :, :], consts["ident"][:, :].unsqueeze(1).broadcast_to([128, 4, 128]), 0.0, None, ALU.mult))
            link(dve.tensor_copy(m.nf[1][:, :, :], m.nf[0][:, :, :].bitcast(FP32)))
            link(dve.tensor_scalar(m.onesR[:, :], consts["ident"][0:DH, :], 0.0, 1.0, ALU.mult, ALU.add))
            for p in range(2):
                link(dve.memset(m.va[p][:, :, :, DH:DH + 1], 1.0))
                for h in range(2):
                    link(dve.memset(m.DR[p][h][:, :, 0:1], 0.0))


def adaln_block(nc, L0_attn_x, L0_attn_Wq, L0_attn_Wkv, L0_attn_Wout, L0_attn_b_out, L0_attn_pos_emb, L0_ffn_gate_w,
                L0_ffn_gate_b, L0_ffn_expert_w, L0_ffn_expert_b, L0_c, L0_wmod, out):
    with ExitStack() as ctx:
        sb = lambda n, s, d=FP32: ctx.enter_context(nc.sbuf_tensor(n, s, d))
        consts = {
            "ident": sb("ident", [128, 128]), "one": sb("one", [128, 1]), "cM": sb("cM", [128, N]),
            "modT": sb("modT", [128, 12, B]),
            "minpos": sb("minpos", [128, 8]),
            "spare": ctx.enter_context(nc.semaphore("spare")),
        }
        flag = sb("flag", [1, 2], I32)
        hT_d = nc.dram_tensor("hT_scratch", [B, 2, 128, KC, N], FP32).ap()
        recip_d = nc.dram_tensor("recip_scratch", [2, 512], FP32).ap()
        attnT_d = nc.dram_tensor("attnT_scratch", [PAIRS, 2, DH, N], FP32).ap()
        gates_d = nc.dram_tensor("gates_scratch", [128, B, 2 * D], FP32).ap()
        prologue(nc, L0_attn_x, L0_c, L0_wmod, hT_d, gates_d, consts)
        with ExitStack() as inner:
            m = Buffers(nc, inner)
            m.one = consts["one"]
            fill(nc, m, L0_attn_pos_emb, consts)
            with nc.Block() as near:
                attention(nc, m, near, hT_d, L0_attn_Wq, L0_attn_Wkv, attnT_d, recip_d, consts, "near", NB=4, W=192, ZW=256)
            coverage(nc, m, consts, flag)
            with nc.Block() as whole:
                attention(nc, m, whole, hT_d, L0_attn_Wq, L0_attn_Wkv, attnT_d, recip_d, consts, "all", NB=1, W=N, ZW=N, guard=flag)
        feed_forward(nc, L0_attn_x, attnT_d, gates_d, (L0_attn_Wout, L0_attn_b_out, L0_ffn_gate_w, L0_ffn_gate_b,
                                              L0_ffn_expert_w, L0_ffn_expert_b), consts, out)


_INS = ['L0_attn_x', 'L0_attn_Wq', 'L0_attn_Wkv', 'L0_attn_Wout', 'L0_attn_b_out', 'L0_attn_pos_emb', 'L0_ffn_gate_w',
        'L0_ffn_gate_b', 'L0_ffn_expert_w', 'L0_ffn_expert_b', 'L0_c', 'L0_wmod']
_OUTS = [((4, 1024, 256), 'float32')]


def kernel(**inputs):
    import numpy as _np
    import concourse.bacc as _bacc
    from concourse import mybir as _mybir
    from concourse.bass_utils import run_bass_kernel_spmd as _run

    nc = _bacc.Bacc("TRN2", target_bir_lowering=False, num_devices=1)
    arrays, args = {}, []
    for name in _INS:
        a = _np.ascontiguousarray(inputs[name])
        arrays[f"in_{name}_dram"] = a
        args.append(nc.dram_tensor(f"in_{name}_dram", a.shape, _mybir.dt.from_np(a.dtype), kind="ExternalInput").ap())
    for i, (shape, dtype) in enumerate(_OUTS):
        dt = _mybir.dt.from_np(_np.dtype(dtype))
        args.append(nc.dram_tensor(f"out_{i}_dram", shape, dt, kind="ExternalOutput").ap())
    adaln_block(nc, *args)
    r = _run(nc, [arrays], core_ids=[0])
    return r.results[0]["out_0_dram"]
```

```python
import concourse.bass as bass
from concourse import mybir
from contextlib import ExitStack

FP32 = mybir.dt.float32
F32R = mybir.dt.float32r
I16 = mybir.dt.int16
I32 = mybir.dt.int32
ALU = mybir.AluOpType
ACT = mybir.ActivationFunctionType
AX = mybir.AxisListType.X

B, N, D = 4, 1024, 256
H, DH = 16, 64
PTS = 64
CAP = float(PTS - 1)
KC = D // 128
TOK = B * N
PAIRS = B * H // 2
NE = 8
THRESHOLD = 0.1
EPS = 1e-5
LOWEST = -3.0e38
MAGIC = 12582912.0
CHUNKS = N // 128
RING = 4


def ge(eng, sem, value):
    if isinstance(value, int) and value <= 0:
        return
    eng.wait_ge(sem, value)


def apart(eng, spare):
    eng.sem_inc(spare)


def prologue(nc, x, c, wmod, hT_d, gates_d, consts):
    ident, modT, cM, spare = (consts[k] for k in ("ident", "modT", "cM", "spare"))
    with ExitStack() as ctx:
        sb = lambda n, s, d=FP32: ctx.enter_context(nc.sbuf_tensor(n, s, d))
        sem = lambda n: ctx.enter_context(nc.semaphore(n))
        wm = sb("wm", [128, KC, 6 * D])
        gates = sb("gates_made", [128, B, 2 * D])
        cT = sb("cT", [128, KC, B])
        en = sb("en", [128, KC, B])
        silu = sb("silu", [128, KC, B])
        siluB = sb("siluB", [128, KC, B, 128])
        sgn = sb("sgn", [128, 512])
        mag = sb("mag", [128, 512])
        cI = sb("cI", [128, N], I32)
        xt = [sb(f"xt{i}", [128, 8, D]) for i in range(2)]
        st = sb("st", [128, 8, 6])
        mv = sb("mv", [128, 8, 2])
        rs = sb("rs", [128, 8])
        xn = sb("xn", [128, 8, D])
        hT = [sb(f"hTa{i}", [128, KC, N]) for i in range(2)]
        eps = sb("eps", [128, 1])
        pm = ctx.enter_context(nc.psum_tensor("pm", [128, 512], FP32))
        pg = [ctx.enter_context(nc.psum_tensor(f"pg{i}", [128, 512], FP32)) for i in range(2)]
        pt = [ctx.enter_context(nc.psum_tensor(f"pt{i}", [128, 512], FP32)) for i in range(4)]
        loaded = sem("a_loaded")
        x_loaded = [sem("a_x_loaded_even"), sem("a_x_loaded_odd")]
        exp_done = sem("a_exp")
        silu_done = sem("a_silu")
        mod_done = sem("a_mod")
        gate_mm = sem("a_gate_mm")
        modT_ready = sem("a_modT")
        chain = sem("a_chain")
        consts_made = sem("a_consts")
        std_done = sem("a_std")
        var_done = sem("a_var")
        norm_done = sem("a_norm")
        tr_done = sem("a_tr")
        h_done = sem("a_h")
        stored = [sem("a_stored_even"), sem("a_stored_odd")]
        gates_stored = sem("a_gates_stored")
        gate_used = sem("a_gate_used")
        block = ctx.enter_context(nc.Block())

        @block.sync
        def _(sp):
            def load(b):
                ge(sp, norm_done, b - 1)
                sp.dma_start(xt[b % 2][:, :, :], x[b].rearrange("(t p) d -> p t d", p=128)).then_inc(x_loaded[b % 2], 16)

            with nc.allow_non_contiguous_dma("1024 floats of the condition, once"):
                for k in range(KC):
                    sp.dma_start(cT[:, k, :], c[:, k * 128:(k + 1) * 128].rearrange("b p -> p b")).then_inc(loaded, 16)
            sp.dma_start(wm[:, :, :], wmod.rearrange("(k p) n -> p k n", p=128)).then_inc(loaded, 16)
            load(0)
            load(1)
            for b in range(B):
                sp.wait_ge(h_done, 4 * b + 4)
                sp.dma_start(hT_d[b], hT[b % 2][:, :, :]).then_inc(stored[b % 2], 16)
                if b + 2 < B:
                    load(b + 2)
            sp.wait_ge(gate_used, B)
            sp.dma_start(gates_d, gates[:, :, :]).then_inc(gates_stored, 16)
            sp.wait_ge(gates_stored, 16)
            for par in range(2):
                sp.wait_ge(stored[par], 16 * B // 2)

        @block.gpsimd
        def _(gp):
            gp.memset(consts["one"][:, :], 1.0).then_inc(consts_made, 1)
            gp.memset(ident[:, :], 0.0).then_inc(consts_made, 1)
            gp.wait_ge(consts_made, 2)
            gp.affine_select(out=ident[:, :], in_=ident[:, :], compare_op=ALU.not_equal, fill=1.0, base=0,
                             pattern=[[-1, 128]], channel_multiplier=1).then_inc(consts_made, 1)
            gp.iota(cI[:, :], pattern=[[-1, N]], base=N - 1, channel_multiplier=0).then_inc(consts_made, 1)
            gp.wait_ge(consts_made, 4)
            gp.tensor_scalar(cM[:, :], cI[:, :], MAGIC, None, ALU.add).then_inc(consts_made, 1)

        @block.scalar
        def _(act):
            act.wait_ge(loaded, 48)
            act.activation(en[:, :, :], cT[:, :, :], ACT.Exp, scale=-1.0).then_inc(exp_done, 1)
            act.wait_ge(modT_ready, 1)
            for b in range(B):
                act.wait_ge(var_done, b + 1)
                act.activation(rs[:, :], mv[:, :, 1], ACT.Sqrt, bias=eps[:, 0:1]).then_inc(std_done, 1)
                ge(act, stored[b % 2], 16 * (b // 2))
                for i in range(4):
                    k = i // 2
                    act.wait_ge(tr_done, 4 * b + i + 1)
                    act.activation(hT[b % 2][:, k, (i % 2) * 512:(i % 2) * 512 + 512], pt[i][:, :], ACT.Identity,
                                   scale=modT[:, 2 + k, b:b + 1], bias=modT[:, k, b:b + 1]).then_inc(h_done, 1)

        @block.tensor
        def _(pe):
            pe.wait_ge(silu_done, 1)
            for ch in range(12):
                for k in range(KC):
                    last = pe.matmul(pm[:, ch * B:(ch + 1) * B], wm[:, k, ch * 128:(ch + 1) * 128], silu[:, k, :],
                                     start=(k == 0), stop=(k == KC - 1))
            last.then_inc(mod_done, 1)
            pe.wait_ge(silu_done, 2)
            pe.wait_ge(consts_made, 3)
            for b in range(B):
                ge(pe, gate_used, b - 1)
                for i, part in enumerate((2, 5)):
                    for k in range(KC):
                        last = pe.matmul(pg[b % 2][:, i * D:(i + 1) * D], siluB[:, k, b, :],
                                         wm[:, k, part * D:(part + 1) * D], start=(k == 0), stop=(k == KC - 1))
                last.then_inc(gate_mm, 1)
                pe.wait_ge(norm_done, b + 1)
                for i in range(4):
                    k, half = i // 2, i % 2
                    ge(pe, h_done, 4 * (b - 1) + i + 1)
                    for t in range(4):
                        last = pe.transpose(pt[i][:, t * 128:(t + 1) * 128],
                                            xn[:, half * 4 + t, k * 128:(k + 1) * 128], ident[:, :])
                    last.then_inc(tr_done, 1)

        @block.vector
        def _(dve):
            done = [0]

            def link(ins):
                done[0] += 1
                ins.then_inc(chain, 1)
                dve.wait_ge(chain, done[0])

            link(dve.memset(eps[:, :], EPS))
            dve.wait_ge(exp_done, 1)
            link(dve.tensor_scalar(en[:, :, :], en[:, :, :], 1.0, None, ALU.add))
            link(dve.reciprocal(en[:, :, :], en[:, :, :]))
            dve.tensor_tensor(silu[:, :, :], cT[:, :, :], en[:, :, :], ALU.mult).then_inc(silu_done, 1)
            dve.wait_ge(silu_done, 1)
            dve.tensor_copy(siluB[:, :, :, :], silu[:, :, :].unsqueeze(3).broadcast_to([128, KC, B, 128])).then_inc(silu_done, 1)
            dve.wait_ge(mod_done, 1)
            link(dve.tensor_copy(modT[:, :, :], pm[:, 0:12 * B].rearrange("p (m b) -> p m b", b=B)))
            link(dve.tensor_scalar(modT[:, 2:4, :], modT[:, 2:4, :], 1.0, None, ALU.add))
            dve.tensor_scalar(modT[:, 8:10, :], modT[:, 8:10, :], 1.0, None, ALU.add).then_inc(modT_ready, 1)
            for b in range(B):
                dve.wait_ge(x_loaded[b % 2], 16 * (b // 2 + 1))
                for t in range(8):
                    last = dve.bn_stats(st[:, t, :], xt[b % 2][:, t, :])
                link(last)
                ge(dve, std_done, b)
                for t in range(8):
                    last = dve.bn_aggr(mv[:, t, :], st[:, t, :])
                last.then_inc(var_done, 1)
                dve.wait_ge(gate_mm, b + 1)
                link(dve.tensor_scalar(sgn[:, :], pg[b % 2][:, :], 0.0, 2.0, ALU.is_ge, ALU.mult))
                link(dve.tensor_scalar(mag[:, :], pg[b % 2][:, :], -1.0, None, ALU.mult))
                link(dve.tensor_tensor(mag[:, :], mag[:, :], pg[b % 2][:, :], ALU.max))
                link(dve.tensor_scalar(mag[:, :], mag[:, :], 0.25, None, ALU.max))
                dve.scalar_tensor_tensor(gates[:, b, :], sgn[:, :], -1.0, mag[:, :], ALU.add, ALU.mult).then_inc(gate_used, 1)
                dve.wait_ge(gate_used, b + 1)
                dve.wait_ge(std_done, b + 1)
                link(dve.reciprocal(rs[:, :], rs[:, :]))
                dve.wait_ge(var_done, b + 1)
                ge(dve, tr_done, 4 * b)
                for t in range(8):
                    last = dve.tensor_scalar(xn[:, t, :], xt[b % 2][:, t, :], mv[:, t, 0:1], rs[:, t:t + 1], ALU.subtract, ALU.mult)
                last.then_inc(norm_done, 1)
                dve.wait_ge(norm_done, b + 1)


def attention(nc, m, blk, hT_d, Wq, Wkv, attnT_d, recip_d, consts, tag, NB, W, ZW, guard=None):
    ident, cM, minpos, spare = (consts[k] for k in ("ident", "cM", "minpos", "spare"))
    IW = NB * 128
    UH = N // IW
    UP = 2 * UH
    UB = 2 * UP
    FAR = N - W
    FCH = (N - ZW) // 128
    EX = ZW - W
    sem = lambda n: m.sem(f"{tag}_{n}")
    S_ready, S_act, S_max = sem("S_ready"), sem("S_act"), sem("S_max")
    A_ready, A_step = sem("A_ready"), sem("A_step")
    fM_read, X_ready, rise_ready = sem("fM_read"), sem("X_ready"), sem("rise_ready")
    B_step = sem("B_step")
    far_bias, z_ready = sem("far_bias"), sem("z_ready")
    row_mm, row_set = sem("row_mm"), sem("row_set")
    T_ready, exp_done, pv_done = sem("T_ready"), sem("exp_done"), sem("pv_done")
    O_copied, sums_turned, recip_made = sem("O_copied"), sem("sums_turned"), sem("recip_made")
    recip_stored, recip_spread, out_ready = sem("recip_stored"), sem("recip_spread"), sem("out_ready")
    stored = [sem("stored_even"), sem("stored_odd")]
    loaded = [sem("loaded_even"), sem("loaded_odd")]
    proj_mm, proj_set, lo_set, D_ready = sem("proj_mm"), sem("proj_set"), sem("lo_set"), sem("D_ready")
    placed = [sem("placed_first"), sem("placed_second")]
    whole_set = sem("whole_set")
    z_shifted, nf_hi, logits_summed = sem("z_shifted"), sem("nf_hi"), sem("logits_summed")
    s16_ready, w_ready, cross_zeroed = sem("s16_ready"), sem("w_ready"), sem("cross_zeroed")
    USES = [("q", 0), ("q", 1), ("k", 0), ("k", 1), ("E", 0), ("v", 0), ("v", 1), ("E", 1)]
    Q_PLACED, PAIR_PLACED = 4 * 16, 12 * 16
    PJ = len(USES)
    SHARE = {1: range(0, 2), 2: range(2, 5), 3: range(5, 8)}
    LEFT = SHARE[3] if UP == 4 else ()

    def v3(t):
        return t[:, 0:NB * W].rearrange("p (t w) -> p t w", w=W)

    Tb, fM, travel = v3(m.Tb), v3(m.fM), v3(m.travel)
    Ps = [v3(t) for t in m.P]
    w_, s16, cross, X = ([v3(t) for t in ts] for ts in (m.w, m.s16, m.cross, m.X))
    mk = [v3(t) for t in m.mk]
    zs = [t[:, 0:NB * ZW].rearrange("p (t w) -> p t w", w=ZW) for t in m.zs]
    fmax, zmax, nfar, negm, mcol = m.fmax, m.zmax, m.nfar, m.negm, m.mcol

    def place(s):
        return s // UP % 2, s % UP // UH, s % UH

    KA = 4
    KM = 12
    KB = KM + 3 + (4 if FAR else 0)
    nbody = PAIRS // 2
    AHEAD = [list(range(NB))[0:1], list(range(NB))[1:2]]
    LATER = [list(range(NB))[2:3], list(range(NB))[3:4]]

    def load_pair(sp, n, pp):
        ge(sp, proj_mm, PJ * (n - 1))
        apart(sp, spare)
        bi, p = n // (H // 2), n % (H // 2)
        sp.dma_start(m.hTb[pp][:, :, :], hT_d[bass.ds(bi, 1)].rearrange("a p k n -> p (a k) n")).then_inc(loaded[pp], 16)
        for which, (src, off) in enumerate(((Wq, 0), (Wkv, 0), (Wkv, H * DH))):
            sp.dma_start(m.wd[pp][:, :, which, :],
                         src.rearrange("(k p) n -> p k n", p=128)[:, :, bass.ds(p * 128 + off, 128)]).then_inc(loaded[pp], 16)

    LD = 4 * 16

    def place_parts(sp, n, pp, i):
        what, half = USES[i]
        cols = slice(half * 512, half * 512 + 512)
        if i == 0:
            ge(sp, T_ready, UP * CHUNKS * (n - 1))
        sp.wait_ge(lo_set, 4 * n + i + 1)
        for h in range(2):
            rows = slice(h * DH, (h + 1) * DH)
            parts = [t[rows, :].bitcast(FP32) for t in (m.hi[half], m.lo[half])]
            for r in range(2):
                to = slice(r * DH, (r + 1) * DH)
                if what == "q":
                    sp.dma_start(m.qs[pp][h][to, cols].bitcast(FP32), parts[r]).then_inc(placed[half], 16)
                else:
                    for part in range(2):
                        sp.dma_start(m.ks[pp][h][part][to, cols].bitcast(FP32), parts[part]).then_inc(placed[half], 16)

    def bank_free(pe, rows, uses):
        ge(pe, row_set, rows)
        ge(pe, proj_set, uses)

    def pe_project(pe, n, pp, i, rows, turn):
        x, w = m.hTb[pp], m.wd[pp]
        bank_free(pe, rows, PJ * n + i)
        if i == 0:
            pe.wait_ge(loaded[pp], LD * turn)
        what, half = USES[i]
        if what in "qk":
            for k in range(KC):
                last = pe.matmul(m.pM[:, :], w[:, k, "qk".index(what), :], x[:, k, half * 512:half * 512 + 512],
                                 start=(k == 0), stop=(k == KC - 1))
        elif what == "v":
            for t in range(4):
                tok = (half * 4 + t) * 128
                for k in range(KC):
                    last = pe.matmul(m.pM[:, t * 128:(t + 1) * 128], x[:, k, tok:tok + 128], w[:, k, 2, :],
                                     start=(k == 0), stop=(k == KC - 1))
        else:
            h = half
            for tokens in range(2):
                pe.wait_ge(placed[tokens], PAIR_PLACED * n + Q_PLACED)
            for t in range(8):
                last = pe.matmul(m.pM[:, t * PTS:(t + 1) * PTS], m.qs[pp][h][:, t * 128:(t + 1) * 128].bitcast(FP32),
                                 m.pos[:, :], start=True, stop=True)
        last.then_inc(proj_mm, 1)

    def pe_scores(pe, g, s, n, tiles):
        pp, h, part = place(s)
        if s % UP == 0 and 0 in tiles:
            for tokens in range(2):
                pe.wait_ge(placed[tokens], PAIR_PLACED * n + PAIR_PLACED)
        for t in tiles:
            i = g * NB + t
            ge(pe, S_act, i - 1)
            if FAR:
                ge(pe, S_max, i - 1)
            for half in range(2):
                for j, ks in enumerate(m.ks[pp][h]):
                    last = pe.matmul(m.pS[(s * NB + t) % 2][:, half * 512:half * 512 + 512],
                                     m.qs[pp][h][:, part * IW + t * 128:part * IW + (t + 1) * 128],
                                     ks[:, half * 512:half * 512 + 512], start=(j == 0), stop=(j == 1))
            last.then_inc(S_ready, 1)

    def pe_values(pe, g, s, uses, between, later, ahead):
        pp, h, part = place(s)
        if FCH:
            pe.wait_ge(far_bias, g + 1)
            bank_free(pe, g, uses)
            for t in range(NB):
                last = pe.matmul(m.pM[:, t * 128:(t + 1) * 128], m.nf[s % 2][:, t, :], m.identR[:, :], start=True, stop=True)
            last.then_inc(row_mm, 1)
            later(0)
            pe.wait_ge(row_set, g + 1)

        def logits(c):
            n = g * CHUNKS + c
            ge(pe, exp_done, n - 1)
            bank = m.pT[c % 2]
            if c < FCH:
                for j, ks in enumerate(m.ks[pp][h]):
                    pe.matmul(bank[:, 0:IW], ks[:, c * 128:(c + 1) * 128], m.qs[pp][h][:, part * IW:(part + 1) * IW],
                              start=(j == 0), stop=False)
                last = pe.matmul(bank[:, 0:IW], m.onesR[:, :], m.rb[:, 0:IW], start=False, stop=True)
            else:
                if c == FCH:
                    pe.wait_ge(z_shifted, g + 1)
                for t in range(NB):
                    last = pe.transpose(bank[:, t * 128:(t + 1) * 128],
                                        zs[s % 4][:, t, (c - FCH) * 128:(c - FCH + 1) * 128], ident[:, :])
            last.then_inc(T_ready, 1)

        logits(0)
        later(1)
        logits(1)
        ge(pe, O_copied, g)
        for c in range(CHUNKS):
            pe.wait_ge(exp_done, g * CHUNKS + c + 1)
            pe.matmul(m.pO[0:DH + 1, 0:IW], m.va[pp][:, c, h, :], m.pr[c % RING][:, 0:IW], start=(c == 0),
                      stop=(c == CHUNKS - 1)).then_inc(pv_done, 1)
            if c + 2 < CHUNKS:
                logits(c + 2)
            between(c)
            if c in (CHUNKS - 3, CHUNKS - 2):
                ahead(c - (CHUNKS - 3))

    def act_scores(act, g, s, tiles):
        if 0 in tiles:
            ge(act, A_ready, g)
            ge(act, T_ready, (g - 3) * CHUNKS)
        for t in tiles:
            act.wait_ge(S_ready, g * NB + t + 1)
            sl = m.pS[(s * NB + t) % 2]
            act.activation(Tb[:, t, :], sl[:, FAR:N], ACT.Tanh, scale=0.5)
            act.activation(zs[s % 4][:, t, :], sl[:, N - ZW:N], ACT.Copy).then_inc(S_act, 1)

    def act_whole(act, g, s):
        par = s % 2
        act.wait_ge(A_ready, g + 1)
        ge(act, z_ready, g - 1)
        act.activation(w_[par], fM, ACT.Identity, bias=m.minus_magic[:, 0:1]).then_inc(whole_set, 1)

    def act_project(act, n, pp, i):
        act.wait_ge(proj_mm, PJ * n + i + 1)
        what, half = USES[i]
        if what in "qk":
            scale = DH ** -0.5 if what == "q" else 1.0
            ge(act, placed[half], PAIR_PLACED * n + (0 if what == "q" else Q_PLACED))
            act.activation(m.raw[half][:, :], m.pM[:, :], ACT.Copy, scale=scale)
            last = act.activation(m.hi[half][:, :], m.pM[:, :], ACT.Copy, scale=scale)
        elif what == "v":
            t = half * 4
            last = act.activation(m.va[pp][:, t:t + 4, :, 0:DH],
                                  m.pM[:, :].rearrange("p (t h d) -> p t h d", t=4, h=2), ACT.Copy)
        else:
            last = act.activation(m.ER[pp][half][:, :, :], m.pM[:, :].rearrange("p (t d) -> p t d", t=8), ACT.Copy)
        last.then_inc(proj_set, 1)

    def act_travel(act, g, s):
        act.wait_ge(fM_read, g + 1)
        ge(act, z_ready, g - 1)
        act.activation(s16[s % 2], travel, ACT.Copy).then_inc(s16_ready, 1)

    def act_values(act, g, s, between, later, ahead, whole, travelled):
        if FCH:
            act.wait_ge(row_mm, g + 1)
            act.activation(m.rb[:, 0:IW], m.pM[0:DH, 0:IW], ACT.Copy).then_inc(row_set, 1)
            later(0)

        def shift():
            act.wait_ge(z_ready, g + 1)
            for t in range(NB):
                z = zs[s % 4]
                if EX:
                    act.activation(z[:, t, 0:EX], z[:, t, 0:EX], ACT.Identity, bias=nfar[s % 2][:, t:t + 1])
                last = act.activation(z[:, t, EX:ZW], z[:, t, EX:ZW], ACT.Identity, bias=negm[s % 2][:, t:t + 1])
            last.then_inc(z_shifted, 1)

        shift_before = max(FCH - 3, 0)
        for c in range(CHUNKS):
            if c == shift_before:
                shift()
            n = g * CHUNKS + c
            act.wait_ge(T_ready, n + 1)
            ge(act, pv_done, n + 1 - RING)
            act.activation(m.pr[c % RING][:, 0:IW], m.pT[c % 2][:, 0:IW], ACT.Exp).then_inc(exp_done, 1)
            if c == 0:
                later(1)
            if c:
                between(c - 1)
            if c == CHUNKS - 4:
                whole()
            if c == CHUNKS - 2:
                ahead(0)
        ahead(1)
        travelled()
        act.wait_ge(pv_done, (g + 1) * CHUNKS)
        ge(act, out_ready, g - 1)
        act.activation(m.oraw[s % 2][:, 0:IW], m.pO[0:DH + 1, 0:IW], ACT.Copy).then_inc(O_copied, 1)

    def pool_table(gp, n, pp, i):
        h = USES[i][1]
        gp.wait_ge(proj_set, PJ * n + i + 1)
        gp.tensor_tensor(m.DR[pp][h][:, :, 1:PTS], m.ER[pp][h][:, :, 0:PTS - 1], m.ER[pp][h][:, :, 1:PTS],
                         ALU.subtract).then_inc(D_ready, 1)
        gp.wait_ge(D_ready, 2 * n + h + 1)

    def pool_low(gp, n, i):
        half = USES[i][1]
        gp.wait_ge(proj_set, PJ * n + i + 1)
        gp.tensor_tensor(m.lo[half][:, :], m.raw[half][:, :], m.hi[half][:, :].bitcast(FP32), ALU.subtract).then_inc(lo_set, 1)

    def pool_project(gp, n, pp, g, uses):
        ge(gp, w_ready, g)
        ge(gp, rise_ready, g - 1)
        ge(gp, out_ready, g - 3)
        for i in uses:
            if USES[i][0] == "E":
                pool_table(gp, n, pp, i)
            elif USES[i][0] in "qk":
                pool_low(gp, n, i)

    def pool_out(gp, g, s):
        gp.wait_ge(recip_spread, 16 * (g + 1))
        ge(gp, stored[s % 2], 16 * (g // 2))
        gp.tensor_tensor(m.oT[s % 2][:, 0:IW], m.oraw[s % 2][0:DH, 0:IW], m.rc[:, 0:IW], ALU.mult).then_inc(out_ready, 1)

    def pool_unit(gp, g, s, n):
        pp, h, part = place(s)
        par = s % 2
        gp.wait_ge(A_ready, g + 1)
        ge(gp, z_ready, g - 1)
        gp.tensor_tensor(cross[par][:, :, 0:W - 1], fM[:, :, 0:W - 1], fM[:, :, 1:W], ALU.subtract)
        ge(gp, s16_ready, g)
        gp.tensor_tensor(travel, cM[:, N - W:N].unsqueeze(1).broadcast_to([128, NB, W]), fM, ALU.subtract).then_inc(fM_read, 1)
        gp.wait_ge(D_ready, 2 * n + h + 1)
        apart(gp, spare)
        for t in range(NB):
            last = gp.tensor_copy(X[par][:, t, :].rearrange("p (r u) -> p r u", u=PTS),
                                  m.DR[pp][h][:, part * NB + t, :].unsqueeze(1).broadcast_to([128, W // PTS, PTS]))
        last.then_inc(X_ready, 1)

    def pool_fraction(gp, g, s):
        gp.wait_ge(whole_set, g + 1)
        gp.tensor_tensor(w_[s % 2], w_[s % 2], Ps[s % 2], ALU.subtract).then_inc(w_ready, 1)

    def pool_rise(gp, g, s):
        par = s % 2
        gp.wait_ge(w_ready, g + 1)
        gp.wait_ge(B_step, KB * g + KM)
        gp.tensor_tensor(w_[par], w_[par], X[par], ALU.mult).then_inc(rise_ready, 1)

    def dve_positions(dve, g, s):
        par = s % 2
        P = Ps[par]

        def scan(t):
            return dve.tensor_tensor_scan(Tb[:, t, ::-1], Tb[:, t, ::-1], m.one[:, 0:1].broadcast_to([128, W]), 0.0,
                                          ALU.add, ALU.add)

        for t in range(NB):
            dve.wait_ge(S_ready, g * NB + t + 1)
            sl = m.pS[(s * NB + t) % 2]
            if FAR:
                dve.reduce_max(fmax[par][:, t:t + 1], sl[:, 0:512], AX)
            dve.wait_ge(S_act, g * NB + t + 1)
            if FAR:
                dve.reduce_max(fmax[par][:, NB + t:NB + t + 1], sl[:, 512:FAR], AX).then_inc(S_max, 1)
            if t:
                scan(t - 1)
        scan(NB - 1).then_inc(A_step, 1)
        dve.wait_ge(A_step, KA * g + 1)
        dve.tensor_scalar(P, Tb, 0.5, CAP, ALU.mult, ALU.min).then_inc(A_step, 1)
        dve.wait_ge(A_step, KA * g + 2)
        dve.tensor_scalar(Tb, P, 0.5, MAGIC, ALU.subtract, ALU.add).then_inc(A_step, 1)
        dve.tensor_tensor(minpos[:, 0:NB], minpos[:, 0:NB], P[:, :, 0], ALU.min).then_inc(A_step, 1)
        ge(dve, fM_read, g)
        ge(dve, whole_set, g)
        dve.wait_ge(A_step, KA * g + 4)
        for t in range(NB):
            last = dve.tensor_tensor_scan(fM[:, t, ::-1], m.one[:, 0:1].broadcast_to([128, W]), Tb[:, t, ::-1],
                                          MAGIC - 1.0, ALU.add, ALU.min)
        last.then_inc(A_ready, 1)
        dve.wait_ge(A_ready, g + 1)

    def dve_logits(dve, g, s, sums):
        pp, h, part = place(s)
        par = s % 2
        x = X[par]
        step = [0]

        def count(ins):
            step[0] += 1
            return ins.then_inc(B_step, 1)

        def after(n):
            dve.wait_ge(B_step, KB * g + n)
            apart(dve, spare)

        def link(ins):
            count(ins)
            dve.wait_ge(B_step, KB * g + step[0])

        def mask(bit):
            count(dve.tensor_scalar(mk[bit % 3], s16[par], 1 << bit, None, ALU.bitwise_and))

        dve.wait_ge(s16_ready, g + 1)
        mask(5)
        mask(4)
        dve.wait_ge(X_ready, g + 1)
        for bit in (5, 4, 3, 2, 1, 0):
            sh = 1 << bit
            after(1 if bit == 5 else 3 + 2 * (4 - bit))
            count(dve.copy_predicated(x[:, :, 0:W - sh], mk[bit % 3][:, :, 0:W - sh], x[:, :, sh:W]))
            if bit >= 2:
                mask(bit - 2)
        assert step[0] == KM
        sums()
        dve.wait_ge(B_step, KB * g + KM)
        cr, P = cross[par], Ps[par]
        if FAR:
            last_entry = m.ER[pp][h][:, part * NB:(part + 1) * NB, 0]
            count(dve.tensor_tensor(mcol[:, 0:NB], fmax[par][:, 0:NB], fmax[par][:, NB:2 * NB], ALU.max))
        ge(dve, cross_zeroed, 2)
        dve.wait_ge(w_ready, g + 1)
        link(dve.tensor_tensor(cr[:, :, 0:W - 1], cr[:, :, 0:W - 1], x[:, :, 1:W], ALU.mult))
        if FAR:
            count(dve.tensor_tensor(mcol[:, 0:NB], mcol[:, 0:NB], last_entry, ALU.add))
        for t in range(NB):
            last = dve.tensor_tensor_scan(P[:, t, ::-1], m.one[:, 0:1].broadcast_to([128, W]), cr[:, t, ::-1],
                                          m.ER[pp][h][:, part * NB + t, PTS - 1:PTS], ALU.mult, ALU.add)
        link(last)
        dve.wait_ge(rise_ready, g + 1)
        link(dve.tensor_tensor(P, P, w_[par], ALU.subtract))
        z = zs[s % 4]
        dve.wait_ge(S_act, (g + 1) * NB)
        apart(dve, spare)
        for t in range(NB):
            last = dve.tensor_tensor_reduce(z[:, t, EX:ZW], z[:, t, EX:ZW], P[:, t, :], 1.0, LOWEST, ALU.add, ALU.max,
                                            zmax[:, t:t + 1])
        last.then_inc(logits_summed, 1)
        dve.wait_ge(logits_summed, g + 1)
        if FAR:
            link(dve.tensor_tensor(mcol[:, 0:NB], mcol[:, 0:NB], zmax[:, 0:NB], ALU.max))
            ge(dve, row_mm, g - 1)
            ge(dve, z_shifted, g - 1)
            link(dve.tensor_tensor(nfar[par][:, 0:NB], last_entry, mcol[:, 0:NB], ALU.subtract))
            dve.tensor_copy(m.nf[par][:, 0:NB, 0], nfar[par][:, 0:NB]).then_inc(nf_hi, 1)
            dve.wait_ge(nf_hi, g + 1)
            dve.tensor_tensor(m.nf[par][:, 0:NB, 32], nfar[par][:, 0:NB], m.nf[par][:, 0:NB, 0].bitcast(FP32),
                              ALU.subtract).then_inc(far_bias, 1)
            top = mcol
        else:
            top = zmax
            ge(dve, z_shifted, g - 1)
        dve.tensor_scalar(negm[par][:, 0:NB], top[:, 0:NB], -1.0, None, ALU.mult).then_inc(z_ready, 1)
        dve.wait_ge(z_ready, g + 1)
        assert step[0] == KB, (step[0], KB)

    def dve_recip(dve, g, s):
        dve.wait_ge(sums_turned, 16 * (g + 1))
        dve.reciprocal(m.rcol[:, 0:NB], m.rcol[:, 0:NB]).then_inc(recip_made, 1)
        dve.wait_ge(recip_made, g + 1)

    def body(eng_slot, it):
        for s in range(UB):
            eng_slot(it, s, it * UB + s)

    def run(eng, slot):
        body(slot, 0)
        with eng.Fori(1, nbody - 1) as it:
            body(slot, it)
        body(slot, nbody - 1)

    def older(it, s, g, back):
        if isinstance(it, int) and it * UB + s < back:
            return None
        return g - back, (s - back) % UB

    def project_at(it, s):
        half, off = s // UP, s % UP
        if off not in SHARE or (isinstance(it, int) and it == nbody - 1 and half == 1):
            return None
        return 2 * it + half + 1, (half + 1) % 2, SHARE[off]

    def unit_ahead(it, s):
        return not (isinstance(it, int) and it == nbody - 1 and s == UB - 1)

    def in_between(eng, pj, step):
        def between(c):
            if pj and c < len(pj[2]):
                step(eng, pj[0], pj[1], pj[2][c])
        return between

    def pe_all(pe):
        for i in range(PJ):
            pe_project(pe, 0, 0, i, 0, 1)
        pe_scores(pe, 0, 0, 0, AHEAD[0] + AHEAD[1])

        def slot(it, s, g):
            n = 2 * it + s // UP
            done_uses = PJ * (2 * it + s // UP + 1) + sum(len(uses) for off, uses in SHARE.items() if off < s % UP)
            if isinstance(it, int) and it == nbody - 1 and s // UP == 1:
                done_uses = PJ * PAIRS
            old = older(it, s, g, 2)
            pj = project_at(it, s)
            PRIOR = (g - 1 if old else 0) if FCH else 0
            between = in_between(pe, pj, lambda e, n, pp, i: pe_project(e, n, pp, i, PRIOR, it + 2 - pp))
            if old:
                pe_values(pe, *old, done_uses, between, lambda i: pe_scores(pe, g, s, n, LATER[i]),
                          lambda i: unit_ahead(it, s) and pe_scores(pe, g + 1, s + 1, 2 * it + (s + 1) // UP, AHEAD[i]))
            else:
                pe_scores(pe, g, s, n, LATER[0] + LATER[1])
                for c in range(CHUNKS):
                    between(c)
                pe_scores(pe, g + 1, s + 1, n, AHEAD[0] + AHEAD[1])
        run(pe, slot)
        for back in (2, 1):
            g = nbody * UB - back
            pe_values(pe, g, g % UB, PJ * PAIRS, lambda c: None, lambda i: None, lambda i: None)

    def act_all(act):
        for i in range(PJ):
            act_project(act, 0, 0, i)
        act_scores(act, 0, 0, AHEAD[0] + AHEAD[1])

        def slot(it, s, g):
            old = older(it, s, g, 2)
            if old:
                act_values(act, *old, in_between(act, project_at(it, s), act_project),
                           lambda i: act_scores(act, g, s, LATER[i]),
                           lambda i: unit_ahead(it, s) and act_scores(act, g + 1, s + 1, AHEAD[i]),
                           lambda: act_whole(act, g, s),
                           lambda: act_travel(act, g, s))
            else:
                act_scores(act, g, s, LATER[0] + LATER[1])
                act_whole(act, g, s)
                act_travel(act, g, s)
                for i in (project_at(it, s) or (0, 0, ()))[2]:
                    act_project(act, *project_at(it, s)[:2], i)
                act_scores(act, g + 1, s + 1, AHEAD[0] + AHEAD[1])
        run(act, slot)
        for back in (2, 1):
            g = nbody * UB - back
            act_values(act, g, g % UB, lambda c: None, lambda i: None, lambda i: None, lambda: None, lambda: None)

    def pool_all(gp):
        for par in range(2):
            gp.memset(cross[par][:, :, W - 1:W], 0.0).then_inc(cross_zeroed, 1)
        gp.wait_ge(cross_zeroed, 2)
        pool_project(gp, 0, 0, 0, range(PJ))

        def slot(it, s, g):
            pj = project_at(it, s - 1) if s else None
            if pj:
                pool_project(gp, pj[0], pj[1], g, pj[2])
            if s == 0 and not (isinstance(it, int) and it == 0):
                pool_project(gp, 2 * it, 0, g, LEFT)
            pool_unit(gp, g, s, 2 * it + s // UP)
            old = older(it, s, g, 1)
            if old:
                pool_rise(gp, *old)
            pool_fraction(gp, g, s)
            old = older(it, s, g, 3)
            if old:
                pool_out(gp, *old)
        run(gp, slot)
        pool_rise(gp, nbody * UB - 1, UB - 1)
        for back in (3, 2, 1):
            g = nbody * UB - back
            pool_out(gp, g, g % UB)

    def dve_all(dve):
        def slot(it, s, g):
            dve_positions(dve, g, s)
            sums = older(it, s, g, 3)
            old = older(it, s, g, 1)
            if old:
                dve_logits(dve, *old, lambda: sums and dve_recip(dve, *sums))
        run(dve, slot)
        G = nbody * UB
        dve_logits(dve, G - 1, (G - 1) % UB, lambda: dve_recip(dve, G - 3, (G - 3) % UB))
        dve_recip(dve, G - 2, (G - 2) % UB)
        dve_recip(dve, G - 1, (G - 1) % UB)

    def sp_sums(sp, g, s):
        sp.wait_ge(O_copied, g + 1)
        sp.dma_start(m.rcol[:, 0:NB], m.oraw[s % 2][DH:DH + 1, 0:IW]).then_inc(sums_turned, 16)

    def sp_spread(sp, g, s):
        sp.wait_ge(recip_made, g + 1)
        sp.dma_start(recip_d[s % 2, 0:IW].rearrange("(p t) -> p t", t=NB), m.rcol[:, 0:NB]).then_inc(recip_stored, 16)
        sp.wait_ge(recip_stored, 16 * (g + 1))
        sp.dma_start(m.rc[:, 0:IW], recip_d[s % 2:s % 2 + 1, 0:IW].broadcast_to([DH, IW])).then_inc(recip_spread, 16)

    def sp_store(sp, n, g, s):
        pp, h, part = place(s)
        sp.wait_ge(out_ready, g + 1)
        apart(sp, spare)
        sp.dma_start(attnT_d[bass.ds(n, 1), h, :, part * IW:(part + 1) * IW].rearrange("a d n -> (a d) n"),
                     m.oT[s % 2][:, 0:IW]).then_inc(stored[s % 2], 16)

    def sp_all(sp):
        load_pair(sp, 0, 0)
        load_pair(sp, 1, 1)
        for i in range(4):
            place_parts(sp, 0, 0, i)

        def slot(it, s, g):
            if s % UP == 0 and not (isinstance(it, int) and it == nbody - 1):
                load_pair(sp, 2 * it + s // UP + 2, s // UP)
            pj = project_at(it, s - 1) if s else None
            for i in (pj[2] if pj else ()):
                if USES[i][0] in "qk":
                    place_parts(sp, pj[0], pj[1], i)
            old = older(it, s, g, 3)
            if old:
                sp_sums(sp, *old)
                sp_spread(sp, *old)
                go, so = old
                sp_store(sp, 2 * it + (s - 3) // UP, go, so)
        run(sp, slot)
        for back in (3, 2, 1):
            g = nbody * UB - back
            sp_sums(sp, g, g % UB)
            sp_spread(sp, g, g % UB)
            sp_store(sp, g // UP, g, g % UB)
        for par in range(2):
            sp.wait_ge(stored[par], 16 * nbody * UB // 2)

    def guarded(eng, work):
        if guard is None:
            work(eng)
        else:
            need = eng.value_load(guard[0:1, 0:1], min_val=0, max_val=128)
            with eng.If(need != 0):
                work(eng)

    @blk.sync
    def _(sp):
        guarded(sp, sp_all)

    @blk.tensor
    def _(pe):
        guarded(pe, pe_all)

    @blk.scalar
    def _(act):
        guarded(act, act_all)

    @blk.gpsimd
    def _(gp):
        guarded(gp, pool_all)

    @blk.vector
    def _(dve):
        guarded(dve, dve_all)


def coverage(nc, m, consts, flag):
    with ExitStack() as ctx:
        minpos, low, low1, ps = consts["minpos"], m.zmax, m.mcol[:, 0:1], m.pM
        compared = ctx.enter_context(nc.semaphore("f_compared"))
        counted = ctx.enter_context(nc.semaphore("f_counted"))
        flagged = ctx.enter_context(nc.semaphore("f_flagged"))
        block = ctx.enter_context(nc.Block())

        @block.vector
        def _(dve):
            dve.tensor_scalar(low[:, :], minpos[:, :], CAP, None, ALU.is_lt).then_inc(compared, 1)
            dve.wait_ge(compared, 1)
            dve.reduce_max(low1, low[:, :], AX).then_inc(compared, 1)
            dve.wait_ge(counted, 1)
            dve.tensor_copy(flag[0:1, 0:1], ps[0:1, 0:1]).then_inc(flagged, 1)
            dve.wait_ge(flagged, 1)

        @block.tensor
        def _(pe):
            pe.wait_ge(compared, 2)
            pe.matmul(ps[0:1, 0:1], low1, consts["one"][:, :], start=True, stop=True).then_inc(counted, 1)


def feed_forward(nc, x, attnT_d, gates_d, weights, consts, out):
    Wout, b_out, gate_w, gate_b, expert_w, expert_b = weights
    ident, modT, spare = (consts[k] for k in ("ident", "modT", "spare"))
    NT = TOK // 128
    with ExitStack() as ctx:
        sb = lambda n, s, d=FP32: ctx.enter_context(nc.sbuf_tensor(n, s, d))
        sem = lambda n: ctx.enter_context(nc.semaphore(n))
        pb = lambda n: ctx.enter_context(nc.psum_tensor(n, [128, 512], FP32))
        wo = sb("wo", [128, H * DH // 128, D])
        gates = sb("gates", [128, B, 2 * D])
        ew = sb("ew", [128, KC, NE, D])
        gw = sb("gw", [128, KC, NE])
        bo = sb("bo", [128, D])
        gb = sb("gb", [128, NE])
        eb = sb("eb", [NE, D])
        aT = [sb(f"aT{i}", [128, H * DH // 128, 128]) for i in range(2)]
        xt = [sb(f"xr{i}", [128, D]) for i in range(2)]
        x1 = [sb(f"x1_{i}", [128, D]) for i in range(2)]
        y = sb("y", [128, D])
        st = sb("st2", [128, 6])
        mv = sb("mv2", [128, 2])
        sd = sb("sd", [128, 1])
        rstd = sb("rstd", [128, 1])
        xn = sb("xn2", [128, D])
        eps = sb("eps2", [128, 1])
        h2T = [sb(f"h2T{i}", [128, KC, 128]) for i in range(2)]
        lg = sb("lg", [128, NE])
        mx = sb("mx", [128, 1])
        ex = sb("ex", [128, NE])
        sm = sb("sm", [128, 1])
        rsm = sb("rsm", [128, 1])
        pr = sb("prg", [128, NE])
        sel = sb("sel", [128, NE])
        ws = sb("ws", [128, 1])
        z0 = sb("z0", [128, 1])
        rws = sb("rws", [128, 1])
        wgt = sb("wgt", [128, NE])
        wT = sb("wT", [NE, 128])
        accs = [sb(f"acc{i}", [128, D]) for i in range(2)]
        res = [sb(f"res{i}", [128, D]) for i in range(2)]
        pY, pH, pG, pB = pb("pY"), pb("pH"), pb("pG"), pb("pB")
        pE = [pb(f"pE{i}") for i in range(4)]
        w_loaded = sem("p_w_loaded")
        in_loaded = [sem("p_in_even"), sem("p_in_odd")]
        y_mm, y_used, x1_made = sem("p_y_mm"), sem("p_y_used"), sem("p_x1")
        chain = sem("p_chain")
        var_done, std_done, norm_done = sem("p_var"), sem("p_std"), sem("p_norm")
        tr_mm, h_set = sem("p_tr"), sem("p_h")
        gate_mm, ex_in, ex_out = sem("p_gate"), sem("p_ex_in"), sem("p_ex_out")
        exp_mm, exp_used = sem("p_experts"), sem("p_experts_used")
        w_made, wT_mm, wT_set, bias_mm, acc_done = sem("p_w"), sem("p_wT"), sem("p_wTs"), sem("p_bias"), sem("p_acc")
        stored = [sem("p_stored_even"), sem("p_stored_odd")]
        acc_summed, gated = sem("p_acc_summed"), sem("p_gated")
        eps_set = sem("p_eps")
        block = ctx.enter_context(nc.Block())
        K1, K2 = 3, 13

        def run(eng, slot):
            for s in range(2):
                slot(0, s, s)
            with eng.Fori(1, NT // 2) as it:
                for s in range(2):
                    slot(it, s, 2 * it + s)

        def tile_before(it, s):
            return not (isinstance(it, int) and it == 0 and s == 0)

        def batch_gate(i, part):
            return gates[:, bass.ds(i // (N // 128), 1), part * D:(part + 1) * D].rearrange("p a d -> p (a d)")

        @block.sync
        def _(sp):
            sp.dma_start(wo[:, :, :], Wout.rearrange("(k p) n -> p k n", p=128)).then_inc(w_loaded, 16)
            for e in range(NE):
                sp.dma_start(ew[:, :, e, :], expert_w[e].rearrange("(k p) n -> p k n", p=128)).then_inc(w_loaded, 16)
            with nc.allow_non_contiguous_dma("small weights, once"):
                sp.dma_start(gw[:, :, :], gate_w.rearrange("(k p) n -> p k n", p=128)).then_inc(w_loaded, 16)
                sp.dma_start(bo[:, :], b_out.rearrange("(a n) -> a n", a=1).broadcast_to([128, D])).then_inc(w_loaded, 16)
                sp.dma_start(gb[:, :], gate_b.rearrange("(a n) -> a n", a=1).broadcast_to([128, NE])).then_inc(w_loaded, 16)
                sp.dma_start(eb[:, :], expert_b).then_inc(w_loaded, 16)
                sp.dma_start(gates[:, :, :], gates_d).then_inc(w_loaded, 16)

            def load(i, par):
                bi, t = i // (N // 128), i % (N // 128)
                ge(sp, x1_made, i - 1)
                apart(sp, spare)
                sp.dma_start(xt[par][:, :], x.rearrange("b n d -> (b n) d")[bass.ds(i * 128, 128), :]).then_inc(in_loaded[par], 16)
                sp.dma_start(aT[par][:, :, :],
                             attnT_d.rearrange("(b k) h d n -> b (h d) k n", b=B)[
                                 bass.ds(bi, 1), :, :, bass.ds(t * 128, 128)].rearrange("a p k n -> p (a k) n")
                             ).then_inc(in_loaded[par], 16)

            def slot(it, s, i):
                load(i, s)
            run(sp, slot)

        @block.gpsimd
        def _(gp):
            def store(i, par):
                gp.wait_ge(acc_summed, i + 1)
                ge(gp, stored[par], 16 * (i // 2))
                apart(gp, spare)
                gp.tensor_tensor(accs[par][:, :], accs[par][:, :], batch_gate(i, 1), ALU.mult).then_inc(gated, 1)
                gp.wait_ge(gated, i + 1)
                gp.tensor_tensor(res[par][:, :], accs[par][:, :], x1[par][:, :], ALU.add).then_inc(acc_done, 1)
                gp.wait_ge(acc_done, i + 1)
                gp.dma_start(out.rearrange("b n d -> (b n) d")[bass.ds(i * 128, 128), :], res[par][:, :]).then_inc(stored[par], 16)

            def slot(it, s, i):
                if tile_before(it, s):
                    store(i - 1, 1 - s)
            gp.wait_ge(w_loaded, 16 * (NE + 6))
            run(gp, slot)
            store(NT - 1, 1)
            for par in range(2):
                gp.wait_ge(stored[par], 16 * NT // 2)

        @block.tensor
        def _(pe):
            pe.wait_ge(w_loaded, 16 * (NE + 6))

            def stage1(it, s, i):
                pe.wait_ge(in_loaded[s], 32 * (it + 1))
                ge(pe, y_used, i)
                for k in range(H * DH // 128):
                    last = pe.matmul(pY[:, 0:D], aT[s][:, k, :], wo[:, k, :], start=(k == 0), stop=(k == H * DH // 128 - 1))
                last.then_inc(y_mm, 1)

            def experts(i, s):
                h = h2T[s]
                pe.wait_ge(h_set, i + 1)
                ge(pe, wT_set, i)
                for k in range(KC):
                    last = pe.matmul(pG[:, 0:NE], h[:, k, :], gw[:, k, :], start=(k == 0), stop=(k == KC - 1))
                last.then_inc(gate_mm, 1)
                for q in range(4):
                    if q == 3:
                        pe.wait_ge(w_made, i + 1)
                        pe.transpose(pG[0:NE, 128:256], wgt[:, :], ident[:, :]).then_inc(wT_mm, 1)
                    ge(pe, exp_used, 4 * (i - 1) + q + 1 if isinstance(i, int) else 4 * i + (q - 3))
                    for k in range(KC):
                        last = pe.matmul(pE[q][:, :], h[:, k, :], ew[:, k, 2 * q:2 * q + 2, :].rearrange("p e n -> p (e n)"),
                                         start=(k == 0), stop=(k == KC - 1))
                    last.then_inc(exp_mm, 1)

            def transposes(i):
                pe.wait_ge(norm_done, i + 1)
                ge(pe, h_set, i)
                for k in range(KC):
                    last = pe.transpose(pH[:, k * 128:(k + 1) * 128], xn[:, k * 128:(k + 1) * 128], ident[:, :])
                last.then_inc(tr_mm, 1)

            def biases(i):
                pe.wait_ge(wT_set, i + 1)
                ge(pe, acc_summed, i)
                pe.matmul(pB[:, 0:D], wT[:, :], eb[:, :], start=True, stop=True).then_inc(bias_mm, 1)

            def slot(it, s, i):
                stage1(it, s, i)
                if tile_before(it, s):
                    experts(i - 1, 1 - s)
                transposes(i)
                if tile_before(it, s):
                    biases(i - 1)
            run(pe, slot)
            experts(NT - 1, 1)
            biases(NT - 1)

        @block.scalar
        def _(act):
            def stage1(i, s):
                act.wait_ge(var_done, i + 1)
                act.activation(sd[:, :], mv[:, 1:2], ACT.Sqrt, bias=eps[:, 0:1]).then_inc(std_done, 1)

            def turned(i, s):
                act.wait_ge(tr_mm, i + 1)
                ge(act, exp_mm, 4 * (i - 1))
                apart(act, spare)
                bi = i // (N // 128)
                for k in range(KC):
                    last = act.activation(h2T[s][:, k, :], pH[:, k * 128:(k + 1) * 128], ACT.Identity,
                                          scale=modT[:, 8 + k, bass.ds(bi, 1)], bias=modT[:, 6 + k, bass.ds(bi, 1)])
                last.then_inc(h_set, 1)

            def exponentials(i):
                act.wait_ge(ex_in, i + 1)
                act.activation(ex[:, :], lg[:, :], ACT.Exp, accum_out=sm[:, :]).then_inc(ex_out, 1)

            def weights_turned(i):
                act.wait_ge(wT_mm, i + 1)
                ge(act, bias_mm, i)
                act.activation(wT[:, :], pG[0:NE, 128:256], ACT.Copy).then_inc(wT_set, 1)

            act.wait_ge(eps_set, 1)

            def slot(it, s, i):
                stage1(i, s)
                if tile_before(it, s):
                    exponentials(i - 1)
                    weights_turned(i - 1)
                turned(i, s)
            run(act, slot)
            exponentials(NT - 1)
            weights_turned(NT - 1)

        @block.vector
        def _(dve):
            dve.memset(eps[:, :], EPS).then_inc(eps_set, 1)
            dve.wait_ge(w_loaded, 16 * (NE + 6))

            def stage1(it, s, i):
                step = [0]

                def link(ins):
                    step[0] += 1
                    ins.then_inc(chain, 1)
                    dve.wait_ge(chain, K1 * i + K2 * (i - 1 if tile_before(it, s) else 0) + step[0])

                dve.wait_ge(in_loaded[s], 32 * (it + 1))
                dve.wait_ge(y_mm, i + 1)
                dve.tensor_tensor(y[:, :], pY[:, 0:D], bo[:, :], ALU.add).then_inc(y_used, 1)
                dve.wait_ge(y_used, i + 1)
                link(dve.tensor_tensor(y[:, :], y[:, :], batch_gate(i, 0), ALU.mult))
                ge(dve, acc_done, i - 1)
                dve.tensor_tensor(x1[s][:, :], y[:, :], xt[s][:, :], ALU.add).then_inc(x1_made, 1)
                dve.wait_ge(x1_made, i + 1)
                link(dve.bn_stats(st[:, :], x1[s][:, :]))
                ge(dve, std_done, i)
                apart(dve, spare)
                dve.bn_aggr(mv[:, :], st[:, :]).then_inc(var_done, 1)
                dve.wait_ge(std_done, i + 1)
                link(dve.reciprocal(rstd[:, :], sd[:, :]))
                ge(dve, tr_mm, i)
                dve.wait_ge(var_done, i + 1)
                dve.tensor_scalar(xn[:, :], x1[s][:, :], mv[:, 0:1], rstd[:, 0:1], ALU.subtract, ALU.mult).then_inc(norm_done, 1)
                dve.wait_ge(norm_done, i + 1)
                assert step[0] == K1

            def stage2(i, s):
                step = [0]

                def link(ins):
                    step[0] += 1
                    ins.then_inc(chain, 1)
                    dve.wait_ge(chain, K1 * (NT if isinstance(i, int) and i == NT - 1 else i + 2) + K2 * i + step[0])

                dve.wait_ge(gate_mm, i + 1)
                link(dve.tensor_tensor(lg[:, :], pG[:, 0:NE], gb[:, :], ALU.add))
                link(dve.reduce_max(mx[:, :], lg[:, :], AX))
                dve.tensor_scalar(lg[:, :], lg[:, :], mx[:, 0:1], None, ALU.subtract).then_inc(ex_in, 1)
                dve.wait_ge(ex_out, i + 1)
                link(dve.reciprocal(rsm[:, :], sm[:, :]))
                link(dve.tensor_scalar(pr[:, :], ex[:, :], rsm[:, 0:1], None, ALU.mult))
                link(dve.scalar_tensor_tensor(sel[:, :], pr[:, :], THRESHOLD, pr[:, :], ALU.is_ge, ALU.mult))
                link(dve.reduce_sum(ws[:, :], sel[:, :], AX))
                link(dve.tensor_scalar(z0[:, :], ws[:, :], 0.0, None, ALU.is_equal))
                link(dve.tensor_tensor(ws[:, :], ws[:, :], z0[:, :], ALU.add))
                link(dve.reciprocal(rws[:, :], ws[:, :]))
                ge(dve, wT_mm, i)
                dve.tensor_scalar(wgt[:, :], sel[:, :], rws[:, 0:1], None, ALU.mult).then_inc(w_made, 1)
                dve.wait_ge(w_made, i + 1)
                acc = accs[s]
                ge(dve, acc_done, i - 1)
                for e in range(NE):
                    if e % 2 == 0:
                        dve.wait_ge(exp_mm, 4 * i + e // 2 + 1)
                    src = pE[e // 2][:, (e % 2) * D:(e % 2 + 1) * D]
                    if e == 0:
                        link(dve.tensor_scalar(acc[:, :], src, wgt[:, 0:1], None, ALU.mult))
                    elif e % 2 == 0:
                        link(dve.scalar_tensor_tensor(acc[:, :], src, wgt[:, e:e + 1], acc[:, :], ALU.mult, ALU.add))
                    else:
                        dve.scalar_tensor_tensor(acc[:, :], src, wgt[:, e:e + 1], acc[:, :], ALU.mult, ALU.add).then_inc(exp_used, 1)
                        dve.wait_ge(exp_used, 4 * i + e // 2 + 1)
                dve.wait_ge(bias_mm, i + 1)
                dve.tensor_tensor(acc[:, :], acc[:, :], pB[:, 0:D], ALU.add).then_inc(acc_summed, 1)
                assert step[0] == K2, step[0]

            def slot(it, s, i):
                stage1(it, s, i)
                if tile_before(it, s):
                    stage2(i - 1, 1 - s)
            run(dve, slot)
            stage2(NT - 1, 1)


class Buffers:

    def __init__(self, nc, ctx):
        sb = lambda n, s, d=FP32: ctx.enter_context(nc.sbuf_tensor(n, s, d))
        pb = lambda n, w=512: ctx.enter_context(nc.psum_tensor(n, [128, w], FP32))
        two = lambda n, s, d=FP32: [sb(f"{n}{i}", s, d) for i in range(2)]
        self.sem = lambda n: ctx.enter_context(nc.semaphore(n))
        self.hTb = two("hTb", [128, KC, N])
        self.wd = two("wd", [128, KC, 3, 128])
        self.raw = two("raw", [128, 512])
        self.hi, self.lo = two("hi", [128, 512], F32R), two("lo", [128, 512], F32R)
        self.qs = [two(f"qs{p}", [128, N], F32R) for p in range(2)]
        self.ks = [[[sb(f"ks{p}{h}{i}", [128, N], F32R) for i in range(2)] for h in range(2)] for p in range(2)]
        self.va = two("va", [128, CHUNKS, 2, DH + 1])
        self.ER = [two(f"ER{p}", [128, CHUNKS, PTS]) for p in range(2)]
        self.DR = [two(f"DR{p}", [128, CHUNKS, PTS]) for p in range(2)]
        self.pos = sb("pos8", [128, PTS])
        self.identR = sb("identR", [128, 128], F32R)
        self.onesR = sb("onesR", [DH, 128], F32R)
        self.nf = two("nf", [128, 4, 128], F32R)
        self.rb = sb("rb", [DH, 512], F32R)
        self.Tb, self.fM, self.travel = (sb(n, [128, N]) for n in ("Tb", "fM", "travel"))
        self.P = two("P", [128, N])
        self.w, self.cross, self.X = two("w", [128, N]), two("cross", [128, N]), two("X", [128, N])
        self.s16, self.mk = two("s16", [128, N], I16), [sb(f"mk{i}", [128, N], I16) for i in range(3)]
        self.zs = [sb(f"zs{i}", [128, N]) for i in range(4)]
        self.fmax, self.nfar, self.negm = two("fmax", [128, 8]), two("nfar", [128, 4]), two("negm", [128, 4])
        self.zmax, self.mcol = sb("zmax", [128, 8]), sb("mcol", [128, 8])
        self.pr = [sb(f"pr{i}", [128, 512]) for i in range(RING)]
        self.oraw, self.rc, self.oT = two("oraw", [DH + 1, 512]), sb("rc", [DH, 512]), two("oT", [DH, 512])
        self.rcol = sb("rcol", [128, 4])
        self.minus_magic = sb("minus_magic", [128, 1])
        self.pS, self.pT = [pb(f"pS{i}", N) for i in range(2)], [pb(f"pT{i}") for i in range(2)]
        self.pO, self.pM = pb("pO"), pb("pM")


def fill(nc, m, pos_emb, consts):
    with ExitStack() as ctx:
        pos = m.pr[0][:, 0:PTS]
        loaded = ctx.enter_context(nc.semaphore("i_loaded"))
        filled = ctx.enter_context(nc.semaphore("i_filled"))
        block = ctx.enter_context(nc.Block())

        @block.sync
        def _(sp):
            for half in range(2):
                sp.dma_start(pos[half * DH:(half + 1) * DH, :], pos_emb).then_inc(loaded, 16)
            sp.wait_ge(loaded, 32)

        @block.vector
        def _(dve):
            done = [0]

            def link(ins):
                done[0] += 1
                ins.then_inc(filled, 1)
                dve.wait_ge(filled, done[0])

            link(dve.memset(consts["minpos"][:, :], CAP + 1.0))
            link(dve.memset(m.minus_magic[:, :], -MAGIC))
            dve.wait_ge(loaded, 32)
            link(dve.tensor_scalar(m.pos[:, :], pos[:, ::-1], float(DH) ** 0.5, None, ALU.mult))
            link(dve.tensor_copy(m.identR[:, :], consts["ident"][:, :]))
            link(dve.tensor_scalar(m.nf[0][:, :, :], consts["ident"][:, :].unsqueeze(1).broadcast_to([128, 4, 128]), 0.0, None, ALU.mult))
            link(dve.tensor_copy(m.nf[1][:, :, :], m.nf[0][:, :, :].bitcast(FP32)))
            link(dve.tensor_scalar(m.onesR[:, :], consts["ident"][0:DH, :], 0.0, 1.0, ALU.mult, ALU.add))
            for p in range(2):
                link(dve.memset(m.va[p][:, :, :, DH:DH + 1], 1.0))
                for h in range(2):
                    link(dve.memset(m.DR[p][h][:, :, 0:1], 0.0))


def adaln_block(nc, L0_attn_x, L0_attn_Wq, L0_attn_Wkv, L0_attn_Wout, L0_attn_b_out, L0_attn_pos_emb, L0_ffn_gate_w,
                L0_ffn_gate_b, L0_ffn_expert_w, L0_ffn_expert_b, L0_c, L0_wmod, out):
    with ExitStack() as ctx:
        sb = lambda n, s, d=FP32: ctx.enter_context(nc.sbuf_tensor(n, s, d))
        consts = {
            "ident": sb("ident", [128, 128]), "one": sb("one", [128, 1]), "cM": sb("cM", [128, N]),
            "modT": sb("modT", [128, 12, B]),
            "minpos": sb("minpos", [128, 8]),
            "spare": ctx.enter_context(nc.semaphore("spare")),
        }
        flag = sb("flag", [1, 2], I32)
        hT_d = nc.dram_tensor("hT_scratch", [B, 128, KC, N], FP32).ap()
        recip_d = nc.dram_tensor("recip_scratch", [2, 512], FP32).ap()
        attnT_d = nc.dram_tensor("attnT_scratch", [PAIRS, 2, DH, N], FP32).ap()
        gates_d = nc.dram_tensor("gates_scratch", [128, B, 2 * D], FP32).ap()
        prologue(nc, L0_attn_x, L0_c, L0_wmod, hT_d, gates_d, consts)
        with ExitStack() as inner:
            m = Buffers(nc, inner)
            m.one = consts["one"]
            fill(nc, m, L0_attn_pos_emb, consts)
            with nc.Block() as near:
                attention(nc, m, near, hT_d, L0_attn_Wq, L0_attn_Wkv, attnT_d, recip_d, consts, "near", NB=4, W=192, ZW=256)
            coverage(nc, m, consts, flag)
            with nc.Block() as whole:
                attention(nc, m, whole, hT_d, L0_attn_Wq, L0_attn_Wkv, attnT_d, recip_d, consts, "all", NB=1, W=N, ZW=N, guard=flag)
        feed_forward(nc, L0_attn_x, attnT_d, gates_d, (L0_attn_Wout, L0_attn_b_out, L0_ffn_gate_w, L0_ffn_gate_b,
                                              L0_ffn_expert_w, L0_ffn_expert_b), consts, out)


_INS = ['L0_attn_x', 'L0_attn_Wq', 'L0_attn_Wkv', 'L0_attn_Wout', 'L0_attn_b_out', 'L0_attn_pos_emb', 'L0_ffn_gate_w',
        'L0_ffn_gate_b', 'L0_ffn_expert_w', 'L0_ffn_expert_b', 'L0_c', 'L0_wmod']
_OUTS = [((4, 1024, 256), 'float32')]


def kernel(**inputs):
    import numpy as _np
    import concourse.bacc as _bacc
    from concourse import mybir as _mybir
    from concourse.bass_utils import run_bass_kernel_spmd as _run

    nc = _bacc.Bacc("TRN2", target_bir_lowering=False, num_devices=1)
    arrays, args = {}, []
    for name in _INS:
        a = _np.ascontiguousarray(inputs[name])
        arrays[f"in_{name}_dram"] = a
        args.append(nc.dram_tensor(f"in_{name}_dram", a.shape, _mybir.dt.from_np(a.dtype), kind="ExternalInput").ap())
    for i, (shape, dtype) in enumerate(_OUTS):
        dt = _mybir.dt.from_np(_np.dtype(dtype))
        args.append(nc.dram_tensor(f"out_{i}_dram", shape, dt, kind="ExternalOutput").ap())
    adaln_block(nc, *args)
    r = _run(nc, [arrays], core_ids=[0])
    return r.results[0]["out_0_dram"]
```
